# Optimizing a Trainium2 kernel written in Bass

```python
import numpy as np
import jax
import jax.numpy as jnp

def _softmax(x, axis=-1):
    return jax.nn.softmax(x, axis=axis)

def _gelu(x):
    return jax.nn.gelu(x, approximate=True)

def _silu(x):
    return jax.nn.silu(x)

def _sigmoid(x):
    return jax.nn.sigmoid(x)

def _layernorm(x, axis=-1, eps=1e-05):
    m = jnp.mean(x, axis=axis, keepdims=True)
    v = jnp.var(x, axis=axis, keepdims=True)
    return (x - m) / jnp.sqrt(v + eps)

def _scatter_add(tgt, idx, src, axis=0):
    return tgt.at[idx].add(src)

def _segment_sum(src, seg, n):
    return jax.ops.segment_sum(src, seg, n)
kernel_name = 'mk_gnn_preln_d1_gnn_r8_ac0864'

def setup_inputs(seed: int=0):
    np.random.seed(seed)
    _w = jnp.asarray

    def _rec_inputs():
        import jax
        import jax.numpy as jnp
        _gk = jax.random.key(seed)
        x = -0.0005121 + 1.001 * jax.random.normal(jax.random.fold_in(_gk, 1), (12500, 64), jnp.float32)
        src = jax.random.randint(jax.random.fold_in(_gk, 2), (200000,), 0, 12500, jnp.int32)
        dst = jnp.minimum((12500 * jax.random.uniform(jax.random.fold_in(_gk, 3), (200000,)) ** 2.0).astype(jnp.int32), 99999)
        _o = jnp.argsort(dst, stable=True)
        src = src[_o]
        dst = dst[_o]
        return (x, src, dst)
    x, src, dst = _rec_inputs()

    def _L0_gnn_setup():
        import jax, jax.numpy as jnp
        import numpy as np
        N_NODES = 6250
        N_EDGES = 100000
        D_FEAT = 64
        D_HID = 128
        key = jax.random.key(seed)
        k_hid, k_w1, k_w2, k_src, k_dst = jax.random.split(key, 5)
        hid = jax.random.normal(k_hid, (N_NODES, D_FEAT), dtype=jnp.float32)
        W1 = jax.random.normal(k_w1, (2 * D_FEAT, D_HID), dtype=jnp.float32) * (1.0 / np.sqrt(2 * D_FEAT))
        b1 = jnp.zeros((D_HID,), dtype=jnp.float32)
        W2 = jax.random.normal(k_w2, (D_HID, D_FEAT), dtype=jnp.float32) * (1.0 / np.sqrt(D_HID))
        b2 = jnp.zeros((D_FEAT,), dtype=jnp.float32)
        src_idx = jax.random.randint(k_src, (N_EDGES,), 0, N_NODES, dtype=jnp.int64 if jax.config.jax_enable_x64 else jnp.int32)
        dst_idx = jax.random.randint(k_dst, (N_EDGES,), 0, N_NODES, dtype=jnp.int64 if jax.config.jax_enable_x64 else jnp.int32)
        return {'hid': hid, 'W1': W1, 'b1': b1, 'W2': W2, 'b2': b2, 'src_idx': src_idx, 'dst_idx': dst_idx}
    _L0_gnn_all = _L0_gnn_setup()
    _L0_gnn_in = {k: v for k, v in _L0_gnn_all.items() if k in ('W1', 'b1', 'W2', 'b2')}
    del _L0_gnn_all
    return {'x': x, 'src': src, 'dst': dst, 'L0_gnn_W1': _L0_gnn_in['W1'], 'L0_gnn_b1': _L0_gnn_in['b1'], 'L0_gnn_W2': _L0_gnn_in['W2'], 'L0_gnn_b2': _L0_gnn_in['b2']}

def reference(x, src, dst, L0_gnn_W1, L0_gnn_b1, L0_gnn_W2, L0_gnn_b2):
    import jax
    import jax.numpy as jnp

    def _L0_gnn_ref(hid, W1, b1, W2, b2, src_idx, dst_idx):
        import jax, jax.numpy as jnp
        import numpy as np
        N_NODES = 6250
        N_EDGES = 100000
        D_FEAT = 64
        D_HID = 128
        n_nodes = hid.shape[0]
        e = jnp.concatenate([hid[src_idx], hid[dst_idx]], axis=1)
        m = jax.nn.relu(e @ W1 + b1) @ W2 + b2
        s = jax.ops.segment_sum(m, dst_idx, num_segments=n_nodes)
        cnt = jax.ops.segment_sum(jnp.ones((m.shape[0],), dtype=m.dtype), dst_idx, num_segments=n_nodes)
        return s / jnp.maximum(cnt, 1.0)[:, None]
    h = jnp.maximum(_layernorm(x, axis=-1), 0.0)
    x = x + _L0_gnn_ref(h, L0_gnn_W1, L0_gnn_b1, L0_gnn_W2, L0_gnn_b2, src, dst)
    return x

_drawn_inputs = setup_inputs


def setup_inputs(seed=0):
    import zlib

    import numpy as np

    out = dict(_drawn_inputs(seed))
    spreads = {'L0_gnn_b1': (0.0, 0.1), 'L0_gnn_b2': (0.0, 0.1)}
    factors = {}
    for name, (base, spread) in spreads.items():
        noise = np.random.default_rng([zlib.crc32(name.encode()), seed]).standard_normal(out[name].shape)
        drawn = base * np.exp(spread * noise) if base else spread * noise
        out[name] = jnp.asarray(drawn.astype(out[name].dtype))
    for name, factor in factors.items():
        out[name] = (out[name] * factor).astype(out[name].dtype)
    return out
```

```python
from contextlib import ExitStack

import concourse.bass as bass
from concourse import mybir

F32 = mybir.dt.float32
BF16 = mybir.dt.bfloat16
I32 = mybir.dt.int32
ALU = mybir.AluOpType
ACT = mybir.ActivationFunctionType
AX = mybir.AxisListType

NODES, FEAT, HID, EDGES = 12500, 64, 128, 200000
EPS = 1e-5

NP = 125
NT = NODES // NP
GT = 10
GROUPS = NT // GT
SPLIT = 112
XT = 20
LOADS = NT // XT
GC = GT * FEAT

WIN = 128
QE = 512
QUADS = -(-EDGES // QE)
FULL = EDGES // QE
REST = EDGES - FULL * QE
CHUNKS = -(-EDGES // 128)
QT = -(-QUADS // 128)
RING = 6
PAD = 65535
MOST = NODES // WIN + 2
ACOLS = 12800
LEAD = 4
BT = 4
BATCHES = NT // BT
PLACES = RING * 4 * HID // (BT * FEAT)
LAG = 3
SRC_BANKS = (0, 1, 2, 7)


def gnn_kernel(nc, x, src, dst, W1, b1, W2, b2, out):
    p_table = nc.dram_tensor("p_table", [NODES, HID], F32).ap()
    q_table = nc.dram_tensor("q_table", [NODES + WIN, HID], F32).ap()

    ctx = ExitStack()
    with ctx:
        def sb(name, shape, dt=F32):
            return ctx.enter_context(nc.sbuf_tensor(name, shape, dt))

        def sem(name):
            return ctx.enter_context(nc.semaphore(name))

        def sems(names):
            return [sem(n) for n in names.split()]

        ident = sb("ident", [128, 128])
        ident16 = sb("ident16", [128, 128], BF16)
        columns = sb("columns", [128, WIN])
        ones16 = sb("ones16", [128, 1], BF16)
        w1 = sb("w1", [128, 2, 2, HID])
        b1_all = sb("b1_all", [NP, HID])
        w2 = sb("w2", [HID, 128])
        b2_all = sb("b2_all", [NP, FEAT])

        xs = sb("xs", [NP, NT, FEAT])
        area = sb("area", [128, ACOLS])
        count = area[0:1, :]

        def of_area(rows, at, k, cols, **dims):
            return area[0:rows, at + k * cols:at + (k + 1) * cols].rearrange("p (a b) -> p a b", **dims)

        centred = [of_area(NP, 0, k, GC, a=GT) for k in (0, 1)]
        squares = [of_area(NP, 2 * GC, k, GC, a=GT) for k in (0, 1)]
        hs = [of_area(NP, 4 * GC, k, GC, a=GT) for k in (0, 1)]
        ht = [of_area(128, 6 * GC, n, NP * GT // 2, a=GT // 2) for n in range(GROUPS)]
        stage = [of_area(NP, 6 * GC + NT * NP // 2, k, GT * HID, a=GT) for k in (0, 1)]
        mean = sb("mean", [NP, NT])
        total = sb("total", [NP, NT])
        stats = sb("stats", [NP, 2, 4, GT])

        acc = sb("acc", [128, ACOLS])
        NE = QT * QE
        src_i, dst_i, src_f, dst_f = (acc[:, k * NE:(k + 1) * NE] for k in range(4))
        src_i, dst_i = (a.bitcast(I32).rearrange("p (t e) -> p t e", t=QT) for a in (src_i, dst_i))
        src_f, dst_f = (a.rearrange("p (t e) -> p t e", t=QT) for a in (src_f, dst_f))
        low = sb("low", [128, QT])
        real = sb("real", [128, QE])
        high = sb("high", [128, QT])
        span = sb("span", [128, QT])
        spans_i = sb("spans_i", [1, QT * 128], I32)
        widest = sb("widest", [1, 1], I32)
        windows_of = sb("windows_of", [1, QT * 128], I32)
        shift = sb("shift", [128, MOST])
        base = sb("base", [128, QT * 128])
        base_i = sb("base_i", [1, QT * 128], I32)
        src_e = sb("src_e", [128, QT * QE], I32)
        rel_e = sb("rel_e", [128, QT * QE])

        idx = sb("idx", [128, RING, 4], I32)
        g = sb("g", [128, RING, 4 * HID])
        qw = sb("qw", [WIN, RING, HID])
        b2_any = g[0:NP, :, :].rearrange("p k (b t f) -> p (k b) t f", t=BT, f=FEAT)
        member = sb("member", [128, 3, 4, WIN])
        member16 = sb("member16", [128, 3, 4, WIN], BF16)
        spread = sb("spread", [WIN, 2, 4, 128])
        z = sb("z", [128, 2, 4 * HID])
        r = sb("r", [128, 2, 4 * HID])
        count_t = sb("count_t", [NP, NT])
        most = sb("most", [NP, NT])
        inverse = sb("inverse", [NP, NT])
        any_edge = sb("any_edge", [NP, NT])
        zero_rows = z[0:WIN, 0, 0:HID]

        bank = [ctx.enter_context(nc.psum_tensor(f"bank{i}", [128, 512], F32)) for i in range(8)]
        z_bank, u_bank, t_bank = bank[0:2], bank[2:4], [bank[4 + k][:, :].bitcast(BF16) for k in (0, 1)]
        h_bank, rows_bank = bank[0:2], [bank[2:5], bank[5:8]]

        rows_ready, rows_in, rows_used, w_loaded, m_made, m_copied, m_turned, m_spread, q_spread, z_made, r_made, \
            u_made, u_added, item_done, all_added = sems(
                "rows_ready rows_in rows_used w_loaded m_made m_copied m_turned m_spread q_spread z_made r_made "
                "u_made u_added item_done all_added")
        high_done, span_done, span_psum, span_done_i, widest_done, windows_shifted, windows_counted, real_done = sems(
            "high_done span_done span_psum span_done_i widest_done windows_shifted windows_counted real_done")

        consts, pads, w1_zero, zeroed, w_in, b1_in, w2_in, b2_in, src_in, dst_in, q_pad = sems(
            "consts pads w1_zero zeroed w_in b1_in w2_in b2_in src_in dst_in q_pad")
        dst_cast, src_cast, low_done, base_psum, base_done, windows, dst_psum, src_psum, dst_table, src_table = sems(
            "dst_cast src_cast low_done base_psum base_done windows dst_psum src_psum dst_table src_table")
        x_in = [sem(f"x_in{n}") for n in range(LOADS)]
        total_done, mean_done, centred_done, sq_done, ss_done, var_done, std_done, rstd_done, h_done = sems(
            "total_done mean_done centred_done sq_done ss_done var_done std_done rstd_done h_done")
        ht_psum, ht_done, p_psum, q_psum, p_staged, q_staged = sems("ht_psum ht_done p_psum q_psum p_staged q_staged")
        p_out, q_out = [sem("p_out0"), sem("p_out1")], [sem("q_out0"), sem("q_out1")]
        u_zero, count_zero = sems("u_zero count_zero")
        idx_ready, member_done, member16_done, t_psum, spread_done, zq_done, z_done, r_done, u_psum, u_done, c_done = \
            sems("idx_ready member_done member16_done t_psum spread_done zq_done z_done r_done u_psum u_done c_done")
        gathered = [sem(f"gathered{k}") for k in range(RING)]
        window_in = [sem(f"window_in{k}") for k in range(RING)]
        count_in, any_done, most_done, inverse_done, b2_scaled, b2_added, o_psum, res_done, out_done = sems(
            "count_in any_done most_done inverse_done b2_scaled b2_added o_psum res_done out_done")

        block = ctx.enter_context(nc.Block())

        x_v = x.rearrange("(p t) f -> p t f", t=NT)
        out_v = out.rearrange("(p t) f -> p t f", t=NT)
        p_v = p_table.rearrange("(p t) h -> p t h", t=NT)
        q_v = q_table[0:NODES, :].rearrange("(p t) h -> p t h", t=NT)

        def columns_of(table, t):
            return table[:, QE * t:QE * (t + 1)].rearrange("e (q c) -> e c q", c=4)

        def tile_of(b):
            return b[:, :].rearrange("e (c q) -> e c q", c=4)

        def parts(rows):
            return [(m, 4 * m, min(4, rows - 4 * m)) for m in range(-(-rows // 4))]

        def rounds(eng, first, last, step):
            whole = (last - first) // RING
            with eng.Fori(0, whole) as i:
                for j in range(first, first + RING):
                    step(i * RING + j, j % RING, i + j // RING)
            for n in range(first + whole * RING, last):
                step(n, n % RING, n // RING)

        def chunks_of(n):
            return CHUNKS - 4 * n if isinstance(n, int) and n == QUADS - 1 else 4

        def if_one_window(eng, fast, general):
            eng.wait_ge(widest_done, 1)
            most_nodes = eng.value_load(widest[0:1, 0:1], min_val=0, max_val=NODES - 1)
            with eng.If(most_nodes < WIN):
                fast()
            with eng.Else():
                general()

        def window_start(eng, low_n, j):
            return nc.s_assert_within(eng.snap(low_n + j * WIN), 0, NODES - 1, skip_runtime_bounds_check_because=
                                      "the quad's windows start at or below its largest dst")

        def items(eng, per_quad, per_window, after=None):
            count_items = eng.alloc_register("items")
            eng.reg_mov(count_items, 1)
            eng.wait_ge(windows_counted, 1)
            with eng.Fori(0, QUADS) as n:
                if per_quad:
                    per_quad(n)
                quad_windows = eng.value_load(windows_of[0:1, bass.ds(n, 1)], min_val=0, max_val=MOST)
                with eng.Fori(0, quad_windows) as j:
                    per_window(n, j, eng.snap(count_items))
                    eng.reg_add(count_items, count_items, 1)
                if after:
                    after(n)
            return eng.snap(count_items)

        def done(n):
            return n + (1 + RING)

        @block.sync
        def _(sp):
            def load_edges(what, to, loaded):
                at = (QT - 1) * 128 * QE
                rows = FULL - (QT - 1) * 128
                sp.dma_start(to[:, 0:QT - 1, :],
                             what[0:at].rearrange("(t p e) -> p t e", p=128, e=QE)).then_inc(loaded, 16)
                sp.dma_start(to[0:rows, QT - 1, :],
                             what[at:at + rows * QE].rearrange("(p e) -> p e", e=QE)).then_inc(loaded, 16)
                sp.dma_start(to[rows:rows + 1, QT - 1, 0:REST],
                             what[FULL * QE:EDGES].rearrange("(p e) -> p e", p=1)).then_inc(loaded, 16)

            for n in range(LOADS):
                s = slice(n * XT, (n + 1) * XT)
                sp.dma_start(xs[0:SPLIT, s, :], x_v[0:SPLIT, s, :]).then_inc(x_in[n], 16)
                sp.dma_start(xs[SPLIT:NP, s, :], x_v[SPLIT:NP, s, :]).then_inc(x_in[n], 16)
                if n == 0:
                    sp.wait_ge(pads, 1)
                    load_edges(dst, dst_i, dst_in)
                if n == 1:
                    sp.wait_ge(pads, 2)
                    load_edges(src, src_i, src_in)

            sp.wait_ge(zeroed, 1)
            sp.dma_start(q_table[NODES:NODES + WIN, :], zero_rows).then_inc(q_pad, 16)
            for table, staged, stored in ((p_v, p_staged, p_out), (q_v, q_staged, q_out)):
                for n in range(GROUPS):
                    s = slice(n * GT, (n + 1) * GT)
                    sp.wait_ge(staged, 3 * (n + 1))
                    sp.dma_start(table[0:SPLIT, s, :], stage[n % 2][0:SPLIT]).then_inc(stored[n % 2], 16)
                    sp.dma_start(table[SPLIT:NP, s, :], stage[n % 2][SPLIT:NP]).then_inc(stored[n % 2], 16)
            for k in (0, 1):
                sp.wait_ge(q_out[k], 16 * GROUPS)
            sp.wait_ge(u_zero, 1)
            sp.dma_start(count.rearrange("o (p c) -> o p c", p=128), acc[:, 0:ACOLS // 128]).then_inc(count_zero, 16)
            sp.wait_ge(q_pad, 16)
            sp.wait_ge(windows, 1)

            def load_window(n, k, use):
                sp.wait_ge(zq_done, done(n - RING))
                at = sp.value_load(base_i[0:1, bass.ds(n, 1)], min_val=0, max_val=NODES - 1)
                sp.dma_start(qw[:, k, :], q_table[bass.ds(at, WIN), :]).then_inc(window_in[k], 16)

            def fast():
                rounds(sp, 0, QUADS, load_window)
                sp.wait_ge(c_done, done(QUADS - 1))

            def general():
                def load_general(n, j, m):
                    low_n = sp.value_load(base_i[0:1, bass.ds(n, 1)], min_val=0, max_val=NODES - 1)
                    at = window_start(sp, low_n, j)
                    sp.wait_ge(item_done, m)
                    sp.dma_start(qw[:, 0, :], q_table[bass.ds(at, WIN), :]).then_inc(w_loaded, 16)

                items(sp, None, load_general)
                sp.wait_ge(all_added, 1)

            if_one_window(sp, fast, general)

            sp.dma_start(count_t[:, :], count[:, 0:NODES].rearrange("o (p t) -> o p t", t=NT)).then_inc(count_in, 16)

            for b in range(0, BATCHES, 5):
                s = slice(BT * b, BT * (b + 5))
                sp.wait_ge(res_done, BT * (b + 5))
                sp.dma_start(out_v[0:SPLIT, s, :], xs[0:SPLIT, s, :]).then_inc(out_done, 16)
                sp.dma_start(out_v[SPLIT:NP, s, :], xs[SPLIT:NP, s, :]).then_inc(out_done, 16)
            sp.wait_ge(out_done, 32 * BATCHES // 5)

        @block.gpsimd
        def _(pool):
            nc.gpsimd.memset(dst_i[:, QT - 1, :], PAD).then_inc(pads, 1)
            nc.gpsimd.memset(src_i[:, QT - 1, :], 0).then_inc(pads, 1)
            nc.gpsimd.memset(w1[:, :, :, :], 0.0).then_inc(w1_zero, 1)
            nc.gpsimd.memset(w2[:, :], 0.0).then_inc(w1_zero, 1)
            nc.gpsimd.memset(ident[:, :], 0.0).then_inc(consts, 1)
            pool.wait_ge(consts, 1)
            nc.gpsimd.affine_select(out=ident[:, :], in_=ident[:, :], compare_op=ALU.not_equal, fill=1.0,
                                    base=0, pattern=[[-1, 128]], channel_multiplier=1).then_inc(consts, 1)
            pool.wait_ge(consts, 2)
            nc.gpsimd.tensor_copy(ident16[:, :], ident[:, :]).then_inc(consts, 1)
            nc.gpsimd.iota(columns[:, :], pattern=[[1, WIN]], base=0, channel_multiplier=0,
                           allow_small_or_imprecise_dtypes=True).then_inc(consts, 1)
            nc.gpsimd.memset(ones16[:, :], 1.0).then_inc(consts, 1)
            nc.gpsimd.memset(zero_rows, 0.0).then_inc(zeroed, 1)

            nc.gpsimd.iota(shift[:, :], pattern=[[WIN, MOST]], base=0, channel_multiplier=0,
                           allow_small_or_imprecise_dtypes=True).then_inc(consts, 1)

            def centre(n):
                s = slice(n * GT, (n + 1) * GT)
                pool.wait_ge(mean_done, n // 2 + 1)
                if n >= 2:
                    pool.wait_ge(h_done, n - 1)
                nc.gpsimd.tensor_tensor(centred[n % 2], xs[:, s, :],
                                        mean[:, s].unsqueeze(2).to_broadcast([NP, GT, FEAT]),
                                        ALU.subtract).then_inc(centred_done, 1)

            for n in range(GROUPS):
                centre(n)
            pool.wait_ge(src_table, QT)
            pool.wait_ge(dst_table, QT)
            nc.gpsimd.memset(acc[:, :], 0.0).then_inc(u_zero, 1)

            pool.wait_ge(p_out[1], 16 * GROUPS)

            def gather(n, k, use):
                ready = pool.to_reg(n + 1)
                pool.wait_ge(p_out[0], 16 * GROUPS)
                pool.wait_ge(idx_ready, ready)
                for j in range(chunks_of(n)):
                    nc.gpsimd.indirect_dma_start(
                        out=g[:, k, j * HID:(j + 1) * HID], out_offset=None, in_=p_table,
                        in_offset=bass.IndirectOffsetOnAxis(ap=idx[:, k, j:j + 1], axis=0)).then_inc(gathered[k], 16)

            def general():
                def gather_general(n):
                    ready = pool.to_reg(n + 1)
                    pool.wait_ge(p_out[0], 16 * GROUPS)
                    pool.wait_ge(rows_ready, ready)
                    for j in range(4):
                        nc.gpsimd.indirect_dma_start(
                            out=g[:, 0, j * HID:(j + 1) * HID], out_offset=None, in_=p_table,
                            in_offset=bass.IndirectOffsetOnAxis(ap=idx[:, 0, j:j + 1], axis=0)).then_inc(rows_in, 16)

                with pool.Fori(0, QUADS) as n:
                    gather_general(n)

            if_one_window(pool, lambda: rounds(pool, 0, QUADS, gather), general)

            for b in range(BATCHES):
                pool.wait_ge(b2_scaled, BT * (b + 1))
                s = slice(BT * b, BT * (b + 1))
                nc.gpsimd.tensor_tensor(xs[:, s, :], xs[:, s, :], b2_any[:, b % PLACES], ALU.add).then_inc(b2_added, 1)

        @block.scalar
        def _(act):
            nc.scalar.preload_act_table(ACT.Sqrt)
            act.dma_start(b1_all[:, :], b1.rearrange("(o h) -> o h", o=1).to_broadcast([NP, HID])).then_inc(b1_in, 16)
            act.dma_start(b2_all[:, :], b2.rearrange("(o f) -> o f", o=1).to_broadcast([NP, FEAT])).then_inc(b2_in, 16)
            act.wait_ge(w1_zero, 2)
            for half in (0, 1):
                act.dma_start(w1[FEAT * half:FEAT * (half + 1), half, :, :],
                              W1.rearrange("(a f) h -> f a h", a=2)).then_inc(w_in, 16)
            act.dma_start(w2[:, 0:FEAT], W2).then_inc(w2_in, 16)

            act.wait_ge(src_in, 48)
            nc.scalar.copy(src_f, src_i).then_inc(src_cast, 1)
            act.wait_ge(base_psum, 1)
            nc.scalar.copy(base[:, :], bank[3][:, :]).then_inc(base_done, 1)
            for t in range(QT):
                act.wait_ge(src_psum, t + 1)
                nc.scalar.copy(columns_of(src_e, t), tile_of(bank[SRC_BANKS[t]])).then_inc(src_table, 1)

            def squares_of(n):
                act.wait_ge(centred_done, n + 1)
                if n >= 2:
                    act.wait_ge(ss_done, n - 1)
                nc.scalar.activation(squares[n % 2], centred[n % 2], ACT.Square).then_inc(sq_done, 1)

            def root_of(n):
                act.wait_ge(var_done, n + 1)
                nc.scalar.activation(stats[:, n % 2, 2, :], stats[:, n % 2, 1, :], ACT.Sqrt).then_inc(std_done, 1)

            def ht_of(n):
                act.wait_ge(ht_psum, n + 1)
                nc.scalar.copy(ht[n][:, 0:4, :],
                               h_bank[0][:, 0:4 * NP].rearrange("p (i n) -> p i n", i=4)).then_inc(ht_done, 1)
                nc.scalar.copy(ht[n][:, 4, :], h_bank[1][:, 0:NP]).then_inc(ht_done, 1)

            def p_of(n):
                act.wait_ge(p_psum, n + 1)
                if n >= 2:
                    act.wait_ge(p_out[n % 2], 32 * (n // 2))
                for m, t, w in parts(GT):
                    nc.scalar.copy(stage[n % 2][:, t:t + w, :],
                                   rows_bank[n % 2][m][0:NP, 0:HID * w].rearrange("p (t h) -> p t h", t=w))\
                        .then_inc(p_staged, 1)

            squares_of(0)
            for n in range(GROUPS + 2):
                if n + 1 < GROUPS:
                    squares_of(n + 1)
                if n < GROUPS:
                    root_of(n)
                if 1 <= n <= GROUPS:
                    ht_of(n - 1)
                if n >= 2:
                    p_of(n - 2)

            for credit in (member16_done, spread_done, r_done):
                act.sem_inc(credit, RING)

            def indices_of(n, k):
                act.wait_ge(z_done, done(n - RING))
                nc.scalar.copy(idx[:, k, :], src_e[:, bass.ds(n * 4, 4)]).then_inc(idx_ready, 1)

            def spread_of(n, k, use):
                act.wait_ge(t_psum, done(n))
                act.wait_ge(zq_done, done(n - 2))
                w = 128 * chunks_of(n)
                nc.scalar.copy(spread[:, k % 2, :, :].rearrange("p c e -> p (c e)")[:, 0:w],
                               t_bank[k % 2][:, 0:w]).then_inc(spread_done, 1)

            def relu(n, k, use):
                w = HID * chunks_of(n)
                act.wait_ge(z_done, done(n))
                act.wait_ge(u_psum, done(n - 2))
                nc.scalar.activation(r[:, k % 2, 0:w], z[:, k % 2, 0:w], ACT.Relu).then_inc(r_done, 1)

            def member16_of(n, k, use):
                act.wait_ge(member_done, done(n))
                act.wait_ge(u_psum, done(n - 3))
                c = chunks_of(n)
                nc.scalar.copy(member16[:, k % 3, 0:c, :], member[:, k % 3, 0:c, :]).then_inc(member16_done, 1)

            def quads(n, k, use):
                here = isinstance(n, int)
                if not here or n + LEAD < QUADS:
                    indices_of(n + LEAD, (k + LEAD) % RING)
                if not here or 1 <= n <= QUADS:
                    spread_of(n - 1, (k - 1) % RING, 0)
                if not here or 2 <= n <= QUADS + 1:
                    relu(n - 2, (k - 2) % RING, 0)
                if not here or n < QUADS:
                    member16_of(n, k, 0)

            def fast():
                for n in range(LEAD):
                    indices_of(n, n)
                for n in range(LAG):
                    quads(n, n, 0)
                rounds(act, LAG, QUADS - LEAD, quads)
                for n in range(QUADS - LEAD, QUADS + LAG):
                    quads(n, n % RING, n // RING)

            def general():
                def indices_general(n):
                    act.wait_ge(rows_used, n + 1)
                    nc.scalar.copy(idx[:, 0, :], src_e[:, bass.ds(n * 4, 4)]).then_inc(rows_ready, 1)

                def window_general(n, j, m):
                    act.wait_ge(m_made, m)
                    nc.scalar.copy(member16[:, 0, :, :], member[:, 0, :, :]).then_inc(m_copied, 1)
                    act.wait_ge(m_turned, m)
                    nc.scalar.copy(spread[:, 0, :, :].rearrange("p c e -> p (c e)"), t_bank[0][:, 0:512])\
                        .then_inc(m_spread, 1)
                    act.wait_ge(z_made, m)
                    nc.scalar.activation(r[:, 0, :], z[:, 0, :], ACT.Relu).then_inc(r_made, 1)

                items(act, indices_general, window_general)

            if_one_window(act, fast, general)

            act.wait_ge(b2_in, 16)
            act.wait_ge(any_done, 1)
            for t in range(NT):
                if t % BT == 0 and t >= BT * PLACES:
                    act.wait_ge(b2_added, t // BT - PLACES + 1)
                nc.scalar.activation(b2_any[:, t // BT % PLACES, t % BT, :], b2_all[:, :], ACT.Copy,
                                     scale=any_edge[:, t:t + 1]).then_inc(b2_scaled, 1)

        @block.vector
        def _(dve):
            def mean_of(n):
                s = slice(n * XT, (n + 1) * XT)
                dve.wait_ge(x_in[n], 32)
                nc.vector.tensor_reduce(total[:, s], xs[:, s, :], AX.X, ALU.add).then_inc(total_done, 1)
                dve.wait_ge(total_done, n + 1)
                nc.vector.tensor_scalar(mean[:, s], total[:, s], 1.0 / FEAT, None, ALU.mult).then_inc(mean_done, 1)

            def normalise(n):
                ss, var, std, rstd = (stats[:, n % 2, m, :] for m in range(4))
                dve.wait_ge(sq_done, n + 1)
                nc.vector.tensor_reduce(ss, squares[n % 2], AX.X, ALU.add).then_inc(ss_done, 1)
                dve.wait_ge(ss_done, n + 1)
                nc.vector.tensor_scalar(var, ss, 1.0 / FEAT, EPS, ALU.mult, ALU.add).then_inc(var_done, 1)
                dve.wait_ge(std_done, n + 1)
                nc.vector.reciprocal(rstd, std).then_inc(rstd_done, 1)
                dve.wait_ge(rstd_done, n + 1)
                if n >= 2:
                    dve.wait_ge(ht_psum, n - 1)
                nc.vector.scalar_tensor_tensor(hs[n % 2], centred[n % 2], 0.0,
                                               rstd.unsqueeze(2).to_broadcast([NP, GT, FEAT]),
                                               ALU.max, ALU.mult).then_inc(h_done, 1)

            def rel_of(t):
                dve.wait_ge(dst_psum, t + 1)
                w = base[:, 128 * t:128 * (t + 1)].rearrange("e (o q) -> e o q", o=1)
                nc.vector.tensor_tensor(columns_of(rel_e, t), tile_of(bank[4 + t % 3]), w.to_broadcast([128, 4, 128]),
                                        ALU.subtract).then_inc(dst_table, 1)

            mean_of(0)
            dve.wait_ge(dst_in, 48)
            nc.vector.tensor_reduce(low[:, :], dst_i, AX.X, ALU.min).then_inc(low_done, 1)
            nc.vector.tensor_copy(dst_f, dst_i).then_inc(dst_cast, 1)
            mean_of(1)
            mean_of(2)
            dve.wait_ge(base_done, 1)
            nc.vector.tensor_copy(base_i[:, :], base[0:1, :]).then_inc(windows, 1)
            dve.wait_ge(dst_cast, 1)
            nc.vector.tensor_reduce(high[:, 0:QT - 1], dst_f[:, 0:QT - 1, :], AX.X, ALU.max)
            nc.vector.scalar_tensor_tensor(real[:, :], dst_f[:, QT - 1, :], float(PAD), dst_f[:, QT - 1, :],
                                           ALU.is_lt, ALU.mult).then_inc(real_done, 1)
            dve.wait_ge(real_done, 1)
            nc.vector.tensor_reduce(high[:, QT - 1:QT], real[:, :], AX.X, ALU.max).then_inc(high_done, 1)
            dve.wait_ge(high_done, 1)
            nc.vector.tensor_tensor(span[:, :], high[:, :], low[:, :], ALU.subtract).then_inc(span_done, 1)
            rel_of(0)
            normalise(0)
            dve.wait_ge(span_psum, 1)
            nc.vector.tensor_copy(spans_i[:, :], bank[3][0:1, :]).then_inc(span_done_i, 1)
            dve.wait_ge(span_done_i, 1)
            nc.vector.tensor_reduce(widest[:, :], spans_i[:, 0:QUADS], AX.X, ALU.max).then_inc(widest_done, 1)
            rel_of(1)
            mean_of(3)
            normalise(1)
            rel_of(2)
            mean_of(4)
            normalise(2)
            rel_of(3)
            for n in range(3, GROUPS):
                normalise(n)

            dve.wait_ge(b1_in, 16)
            for n in range(GROUPS):
                dve.wait_ge(q_psum, n + 1)
                if n < 2:
                    dve.wait_ge(p_out[n], 16 * GROUPS)
                else:
                    dve.wait_ge(q_out[n % 2], 32 * (n // 2))
                for m, t, w in parts(GT):
                    nc.vector.tensor_tensor(stage[n % 2][:, t:t + w, :],
                                            rows_bank[n % 2][m][0:NP, 0:HID * w].rearrange("p (t h) -> p t h", t=w),
                                            b1_all[:, :].unsqueeze(1).to_broadcast([NP, w, HID]),
                                            ALU.add).then_inc(q_staged, 1)

            dve.wait_ge(q_pad, 16)
            for credit in (member_done, z_done, u_done, c_done):
                dve.sem_inc(credit, RING)

            def members_of(n, k, use):
                dve.wait_ge(u_psum, done(n - 3))
                dve.wait_ge(member16_done, done(n - 3))
                for j in range(chunks_of(n)):
                    last = nc.vector.tensor_scalar(member[:, k % 3, j, :], columns[:, :],
                                                   rel_e[:, bass.ds(n * 4 + j, 1)], None, ALU.is_equal)
                last.then_inc(member_done, 1)

            def add_rows(n, k, use):
                w = HID * chunks_of(n)
                dve.wait_ge(zq_done, done(n))
                dve.wait_ge(gathered[k], use * 64 + 16 * chunks_of(n))
                dve.wait_ge(r_done, done(n - 2))
                nc.vector.tensor_tensor(z[:, k % 2, 0:w], z_bank[k % 2][:, 0:w], g[:, k, 0:w],
                                        ALU.add).then_inc(z_done, 1)

            def add_sums(n, k, use):
                at = dve.value_load(base_i[0:1, bass.ds(n, 1)], min_val=0, max_val=NODES - 1)
                u, c = acc[:, bass.ds(at, WIN)], count[:, bass.ds(at, WIN)]
                sums = u_bank[k % 2]
                dve.wait_ge(u_psum, done(n))
                dve.wait_ge(u_done, done(n - 1))
                dve.wait_ge(c_done, done(n - 1))
                nc.vector.tensor_tensor(u, u, sums[:, 0:WIN], ALU.add).then_inc(u_done, 1)
                nc.vector.tensor_tensor(c, c, sums[0:1, WIN:2 * WIN], ALU.add).then_inc(c_done, 1)

            def quads(n, k, use):
                here = isinstance(n, int)
                if not here or 2 <= n <= QUADS + 1:
                    add_rows(n - 2, (k - 2) % RING, use - (1 if k < 2 else 0))
                if here and n == 3:
                    dve.wait_ge(count_zero, 16)
                    dve.wait_ge(u_zero, 1)
                if not here or n >= 3:
                    add_sums(n - 3, (k - 3) % RING, 0)
                if not here or n < QUADS:
                    members_of(n, k, 0)

            def fast():
                for n in range(LAG):
                    quads(n, n, 0)
                rounds(dve, LAG, QUADS - LEAD, quads)
                for n in range(QUADS - LEAD, QUADS + LAG):
                    quads(n, n % RING, n // RING)

            def general():
                dve.wait_ge(span_done_i, 1)
                nc.vector.tensor_scalar(windows_of[:, :], spans_i[:, :], WIN.bit_length() - 1, None,
                                        ALU.arith_shift_right).then_inc(windows_shifted, 1)
                dve.wait_ge(windows_shifted, 1)
                nc.vector.tensor_scalar(windows_of[:, :], windows_of[:, :], 1, None, ALU.add)\
                    .then_inc(windows_counted, 1)
                dve.wait_ge(count_zero, 16)
                dve.wait_ge(u_zero, 1)
                dve.sem_inc(item_done, 1)
                dve.sem_inc(rows_used, 1)

                def window_general(n, j, m):
                    low_n = dve.value_load(base_i[0:1, bass.ds(n, 1)], min_val=0, max_val=NODES - 1)
                    at = window_start(dve, low_n, j)
                    u, c = acc[:, bass.ds(at, WIN)], count[:, bass.ds(at, WIN)]
                    gathers = dve.to_reg((n + 1) * 64)
                    dve.wait_ge(item_done, m)
                    for k in range(4):
                        last = nc.vector.tensor_scalar(member[:, 0, k, :], columns[:, :], shift[:, bass.ds(j, 1)],
                                                       rel_e[:, bass.ds(n * 4 + k, 1)], ALU.add, ALU.is_equal)
                    last.then_inc(m_made, 1)
                    dve.wait_ge(q_spread, m)
                    dve.wait_ge(rows_in, gathers)
                    nc.vector.tensor_tensor(z[:, 0, :], z_bank[0][:, :], g[:, 0, :], ALU.add).then_inc(z_made, 1)
                    dve.wait_ge(u_made, m)
                    nc.vector.tensor_tensor(u, u, u_bank[0][:, 0:WIN], ALU.add).then_inc(u_added, 1)
                    dve.wait_ge(u_added, m)
                    nc.vector.tensor_tensor(c, c, u_bank[0][0:1, WIN:2 * WIN], ALU.add).then_inc(item_done, 1)

                def quad_done(n):
                    dve.sem_inc(rows_used, 1)

                dve.wait_ge(item_done, items(dve, None, window_general, quad_done))
                dve.sem_inc(all_added, 1)

            if_one_window(dve, fast, general)

            dve.wait_ge(count_in, 16)
            nc.vector.tensor_scalar(any_edge[:, :], count_t[:, :], 1.0, None, ALU.min).then_inc(any_done, 1)
            nc.vector.tensor_scalar(most[:, :], count_t[:, :], 1.0, None, ALU.max).then_inc(most_done, 1)
            dve.wait_ge(most_done, 1)
            nc.vector.reciprocal(inverse[:, :], most[:, :]).then_inc(inverse_done, 1)
            dve.wait_ge(inverse_done, 1)
            for b in range(BATCHES):
                dve.wait_ge(o_psum, b + 1)
                dve.wait_ge(b2_added, b + 1)
                for t in range(BT * b, BT * (b + 1)):
                    nc.vector.scalar_tensor_tensor(xs[:, t, :], bank[b % 8][0:NP, 128 * (t % BT):128 * (t % BT) + FEAT],
                                                   inverse[:, t:t + 1], xs[:, t, :],
                                                   ALU.mult, ALU.add).then_inc(res_done, 1)

        @block.tensor
        def _(pe):
            def transposed(table, t, to, psum):
                for c in range(4):
                    last = nc.tensor.transpose(to[:, 128 * c:128 * (c + 1)], table[:, t, 128 * c:128 * (c + 1)],
                                               ident[:, :])
                last.then_inc(psum, 1)

            pe.wait_ge(consts, 5)
            pe.wait_ge(low_done, 1)
            for t in range(QT):
                last = nc.tensor.matmul(bank[3][:, 128 * t:128 * (t + 1)], low[:, t:t + 1].to_broadcast([128, 128]),
                                        ident[:, :], start=True, stop=True)
            last.then_inc(base_psum, 1)
            pe.wait_ge(dst_cast, 1)
            for t in range(QT):
                if t == 3:
                    pe.wait_ge(dst_table, 1)
                transposed(dst_f, t, bank[4 + t % 3], dst_psum)

            pe.wait_ge(span_done, 1)
            pe.wait_ge(base_done, 1)
            for t in range(QT):
                last = nc.tensor.matmul(bank[3][0:1, 128 * t:128 * (t + 1)], span[:, t:t + 1], ident[:, :],
                                        start=True, stop=True)
            last.then_inc(span_psum, 1)
            pe.wait_ge(src_cast, 1)
            for t in range(QT):
                transposed(src_f, t, bank[SRC_BANKS[t]], src_psum)

            def transpose_h(n):
                pe.wait_ge(h_done, n + 1)
                if n:
                    pe.wait_ge(ht_done, 2 * n)
                for i in range(GT // 2):
                    last = nc.tensor.transpose(h_bank[i // 4][:, NP * (i % 4):NP * (i % 4 + 1)],
                                               hs[n % 2][:, 2 * i:2 * i + 2, :].rearrange("p t f -> p (t f)"),
                                               ident[0:NP, 0:NP])
                last.then_inc(ht_psum, 1)

            def products(n, half, psum):
                for t in range(GT):
                    last = nc.tensor.matmul(rows_bank[n % 2][t // 4][0:NP, HID * (t % 4):HID * (t % 4 + 1)],
                                            ht[n][:, t // 2, :], w1[:, t % 2, half, :], start=True, stop=True)
                last.then_inc(psum, 1)

            pe.wait_ge(w_in, 32)
            pe.wait_ge(src_table, QT)
            for n in range(GROUPS + 1):
                if n < GROUPS:
                    transpose_h(n)
                if n:
                    if n == 1:
                        pe.wait_ge(span_done_i, 1)
                        pe.wait_ge(dst_table, QT)
                    if n == 2:
                        pe.wait_ge(dst_table, QT)
                    pe.wait_ge(ht_done, 2 * n)
                    if n > 2:
                        pe.wait_ge(p_staged, 3 * (n - 2))
                    products(n - 1, 0, p_psum)
            for n in range(GROUPS):
                if n < 2:
                    pe.wait_ge(p_staged, 3 * (GROUPS - 1 + n))
                else:
                    pe.wait_ge(q_staged, 3 * (n - 1))
                products(n, 1, q_psum)

            pe.wait_ge(q_staged, 3 * GROUPS)
            for credit in (t_psum, zq_done, u_psum):
                pe.sem_inc(credit, RING)

            def spread_q(n, k, use):
                pe.wait_ge(spread_done, done(n))
                pe.wait_ge(window_in[k], use * 16 + 16)
                pe.wait_ge(z_done, done(n - 2))
                for j in range(chunks_of(n)):
                    last = nc.tensor.matmul(z_bank[k % 2][:, HID * j:HID * (j + 1)], spread[:, k % 2, j, :],
                                            qw[:, k, :], start=True, stop=True)
                last.then_inc(zq_done, 1)

            def sum_edges(n, k, use):
                pe.wait_ge(r_done, done(n))
                pe.wait_ge(c_done, done(n - 2))
                sums = u_bank[k % 2]
                chunks = chunks_of(n)
                for c in range(chunks):
                    nc.tensor.matmul(sums[:, 0:WIN], r[:, k % 2, HID * c:HID * (c + 1)], member[:, k % 3, c, :],
                                     start=c == 0, stop=c == chunks - 1)
                for c in range(chunks):
                    last = nc.tensor.matmul(sums[0:1, WIN:2 * WIN], ones16[:, :], member16[:, k % 3, c, :],
                                            start=c == 0, stop=c == chunks - 1)
                last.then_inc(u_psum, 1)

            def transpose_members(n, k, use):
                pe.wait_ge(member16_done, done(n))
                pe.wait_ge(spread_done, done(n - 2))
                for c in range(chunks_of(n)):
                    last = nc.tensor.transpose(t_bank[k % 2][:, 128 * c:128 * (c + 1)], member16[:, k % 3, c, :],
                                               ident16[:, :])
                last.then_inc(t_psum, 1)

            def quads(n, k, use):
                here = isinstance(n, int)
                if not here or 1 <= n <= QUADS:
                    spread_q(n - 1, (k - 1) % RING, use - (0 if k else 1))
                if not here or 2 <= n <= QUADS + 1:
                    sum_edges(n - 2, (k - 2) % RING, 0)
                if not here or n < QUADS:
                    transpose_members(n, k, 0)

            def fast():
                for n in range(LAG):
                    quads(n, n, 0)
                rounds(pe, LAG, QUADS - LEAD, quads)
                for n in range(QUADS - LEAD, QUADS + LAG):
                    quads(n, n % RING, n // RING)
                pe.wait_ge(u_done, done(QUADS - 1))
                pe.wait_ge(c_done, done(QUADS - 1))

            def general():
                def window_general(n, j, m):
                    loads = pe.to_reg(m * 16)
                    pe.wait_ge(m_copied, m)
                    for c in range(4):
                        last = nc.tensor.transpose(t_bank[0][:, 128 * c:128 * (c + 1)], member16[:, 0, c, :],
                                                   ident16[:, :])
                    last.then_inc(m_turned, 1)
                    pe.wait_ge(m_spread, m)
                    pe.wait_ge(w_loaded, loads)
                    for c in range(4):
                        last = nc.tensor.matmul(z_bank[0][:, HID * c:HID * (c + 1)], spread[:, 0, c, :], qw[:, 0, :],
                                                start=True, stop=True)
                    last.then_inc(q_spread, 1)
                    pe.wait_ge(r_made, m)
                    for c in range(4):
                        nc.tensor.matmul(u_bank[0][:, 0:WIN], r[:, 0, HID * c:HID * (c + 1)], member[:, 0, c, :],
                                         start=c == 0, stop=c == 3)
                    for c in range(4):
                        last = nc.tensor.matmul(u_bank[0][0:1, WIN:2 * WIN], ones16[:, :], member16[:, 0, c, :],
                                                start=c == 0, stop=c == 3)
                    last.then_inc(u_made, 1)

                items(pe, None, window_general)
                pe.wait_ge(all_added, 1)

            if_one_window(pe, fast, general)

            pe.wait_ge(w2_in, 16)
            for b in range(BATCHES):
                if b >= 8:
                    pe.wait_ge(res_done, BT * (b - 7))
                for t in range(BT):
                    node = slice(BT * b + t, BT * b + t + (NP - 1) * NT + 1, NT)
                    last = nc.tensor.matmul(bank[b % 8][0:NP, 128 * t:128 * (t + 1)], acc[:, node], w2[:, :],
                                            start=True, stop=True)
                last.then_inc(o_psum, 1)


_INS = ["x", "src", "dst", "L0_gnn_W1", "L0_gnn_b1", "L0_gnn_W2", "L0_gnn_b2"]


def kernel(**inputs):
    import numpy as _np
    import concourse.bacc as _bacc
    from concourse import mybir as _mybir
    from concourse.bass_utils import run_bass_kernel_spmd as _run

    nc = _bacc.Bacc("TRN2", target_bir_lowering=False, num_devices=1)
    arrays, args = {}, []
    for name in _INS:
        a = _np.ascontiguousarray(inputs[name])
        arrays[f"in_{name}_dram"] = a
        args.append(nc.dram_tensor(f"in_{name}_dram", a.shape, _mybir.dt.from_np(a.dtype), kind="ExternalInput").ap())
    out = nc.dram_tensor("out_0_dram", [NODES, FEAT], F32, kind="ExternalOutput").ap()
    gnn_kernel(nc, *args, out)
    r = _run(nc, [arrays], core_ids=[0])
    return r.results[0]["out_0_dram"]
```

```python
from contextlib import ExitStack

import concourse.bass as bass
from concourse import mybir

F32 = mybir.dt.float32
BF16 = mybir.dt.bfloat16
I32 = mybir.dt.int32
ALU = mybir.AluOpType
ACT = mybir.ActivationFunctionType
AX = mybir.AxisListType

NODES, FEAT, HID, EDGES = 12500, 64, 128, 200000
EPS = 1e-5

NP = 125
NT = NODES // NP
GT = 10
GROUPS = NT // GT
SPLIT = 112
XT = 20
LOADS = NT // XT
GC = GT * FEAT

WIN = 128
QE = 512
QUADS = -(-EDGES // QE)
FULL = EDGES // QE
REST = EDGES - FULL * QE
CHUNKS = -(-EDGES // 128)
QT = -(-QUADS // 128)
RING = 12
PAD = 65535
MOST = NODES // WIN + 2
ACOLS = 12800
LEAD = 9
MEMBERS = 4
BT = 4
BATCHES = NT // BT
STORES = (0, 6, 12, 18, 23, BATCHES)
PLACES = RING * 4 * HID // (BT * FEAT)
POOL_BATCHES = 4
EARLY = 4
LAG = 3
CENTRED, HS, STAGES = 4, 3, 3


def gnn_kernel(nc, x, src, dst, W1, b1, W2, b2, out):
    p_table = nc.dram_tensor("p_table", [NODES, HID], F32).ap()
    q_table = nc.dram_tensor("q_table", [NODES + WIN, HID], F32).ap()

    ctx = ExitStack()
    with ctx:
        def sb(name, shape, dt=F32):
            return ctx.enter_context(nc.sbuf_tensor(name, shape, dt))

        def sem(name):
            return ctx.enter_context(nc.semaphore(name))

        def sems(names):
            return [sem(n) for n in names.split()]

        ident = sb("ident", [128, 128])
        ident16 = sb("ident16", [128, 128], BF16)
        columns = sb("columns", [128, WIN])
        ones16 = sb("ones16", [128, 1], BF16)
        w1 = sb("w1", [128, 2, 2, HID])
        b1_all = sb("b1_all", [NP, HID])
        w2 = sb("w2", [HID, 128])
        b2_all = sb("b2_all", [NP, FEAT])

        xs = sb("xs", [NP, NT, FEAT])
        area = sb("area", [128, ACOLS])
        count = area[0:1, :]

        def of_area(rows, at, k, cols, **dims):
            return area[0:rows, at + k * cols:at + (k + 1) * cols].rearrange("p (a b) -> p a b", **dims)

        hs = [of_area(NP, 0, k, GC, a=GT) for k in range(HS)]
        ht = [of_area(128, HS * GC, n, NP * GT // 2, a=GT // 2) for n in range(GROUPS)]
        stage = [of_area(NP, HS * GC + NT * NP // 2, k, GT * HID, a=GT) for k in range(STAGES)]
        mean = sb("mean", [NP, NT])
        total = sb("total", [NP, NT])
        stats = sb("stats", [NP, 2, 3, GT])
        eps = sb("eps", [NP, 1])

        acc = sb("acc", [128, ACOLS])
        NE = QT * QE
        src_i, dst_i, src_f, dst_f = (acc[:, k * NE:(k + 1) * NE] for k in range(4))
        src_i, dst_i = (a.bitcast(I32).rearrange("p (t e) -> p t e", t=QT) for a in (src_i, dst_i))
        src_f, dst_f = (a.rearrange("p (t e) -> p t e", t=QT) for a in (src_f, dst_f))
        low = sb("low", [128, QT])
        high = sb("high", [128, QT])
        span = sb("span", [128, QT])
        spans_i = sb("spans_i", [1, QT * 128], I32)
        widest = sb("widest", [1, 1], I32)
        shift = sb("shift", [128, MOST])
        base = sb("base", [128, QT * 128])
        base_i = sb("base_i", [1, QT * 128], I32)
        src_e = sb("src_e", [128, QT * QE], I32)
        rel_e = sb("rel_e", [128, QT * QE])

        idx = sb("idx", [128, RING, 4], I32)
        g = sb("g", [128, RING, 4 * HID])
        qw = sb("qw", [WIN, RING, HID])
        rows = g[:, :, :].rearrange("p k c -> p (k c)")
        b2_any = rows[0:NP, :].rearrange("p (b t f) -> p b t f", t=BT, f=FEAT)
        centred = [rows[0:NP, k * GC:(k + 1) * GC].rearrange("p (t f) -> p t f", t=GT) for k in range(CENTRED)]
        windows_of = g[0:1, 1, :].bitcast(I32)
        member = sb("member", [128, MEMBERS, 4, WIN])
        squares = member[0:NP, 0:3, :, :].rearrange("p k c w -> p (k c w)")[:, 0:2 * GC] \
            .rearrange("p (k t f) -> p k t f", k=2, t=GT)
        member16 = sb("member16", [128, MEMBERS, 4, WIN], BF16)
        spread = sb("spread", [WIN, 2, 4, 128])
        z = sb("z", [128, 2, 4 * HID])
        r = sb("r", [128, 2, 4 * HID])
        count_t = sb("count_t", [NP, NT])
        most, inverse, any_edge = mean, total, b1_all[:, 0:NT]
        zeros = spread[:, 1, 3, :]
        real = r[:, 0, :]

        bank = [ctx.enter_context(nc.psum_tensor(f"bank{i}", [128, 512], F32)) for i in range(8)]
        z_bank, u_bank, t_bank = bank[0:2], bank[2:4], [bank[4 + k][:, :].bitcast(BF16) for k in (0, 1)]
        c_bank = bank[6:8]
        h_bank, rows_bank = bank[0:2], [bank[2:5], bank[5:8]]

        rows_ready, rows_in, rows_used, w_loaded, m_made, m_copied, m_turned, m_spread, q_spread, z_made, r_made, \
            u_made, u_added, item_done, all_added = sems(
                "rows_ready rows_in rows_used w_loaded m_made m_copied m_turned m_spread q_spread z_made r_made "
                "u_made u_added item_done all_added")
        high_done, real_done, span_done, span_psum, span_done_i, widest_done, windows_shifted, windows_counted = sems(
            "high_done real_done span_done span_psum span_done_i widest_done windows_shifted windows_counted")
        eps_there = sem("eps_there")

        consts, pads, w1_zero, zeroed, w_in, b1_in, w2_in, b2_in, src_in, dst_in, q_pad = sems(
            "consts pads w1_zero zeroed w_in b1_in w2_in b2_in src_in dst_in q_pad")
        dst_cast, src_cast, low_done, base_psum, base_done, windows, dst_psum, src_psum, dst_table, src_table = sems(
            "dst_cast src_cast low_done base_psum base_done windows dst_psum src_psum dst_table src_table")
        x_in = [sem(f"x_in{n}") for n in range(LOADS)]
        total_done, mean_done, centred_done, sq_done, ss_done, std_done, rstd_done, h_done = sems(
            "total_done mean_done centred_done sq_done ss_done std_done rstd_done h_done")
        ht_psum, ht_done, p_psum, q_psum, p_staged, q_staged = sems("ht_psum ht_done p_psum q_psum p_staged q_staged")
        p_out, q_out = ([sem(f"{table}_out{k}") for k in range(STAGES)] for table in "pq")
        all_out = [32 * len(range(k, GROUPS, STAGES)) for k in range(STAGES)]
        q_all_out = [32 * len(range((k - GROUPS) % STAGES, GROUPS, STAGES)) for k in range(STAGES)]
        u_zero, count_zero = sems("u_zero count_zero")
        idx_ready, member_done, member16_done, t_psum, c_psum, spread_done, zq_done, z_done, r_done, u_psum, u_done, \
            c_done = sems("idx_ready member_done member16_done t_psum c_psum spread_done zq_done z_done r_done u_psum "
                          "u_done c_done")
        gathered = [sem(f"gathered{k}") for k in range(RING)]
        window_in = [sem(f"window_in{k}") for k in range(RING)]
        count_in, any_done, most_done, inverse_done, b2_first, b2_scaled, b2_added, o_psum, res_done, out_done = sems(
            "count_in any_done most_done inverse_done b2_first b2_scaled b2_added o_psum res_done out_done")

        block = ctx.enter_context(nc.Block())

        x_v = x.rearrange("(p t) f -> p t f", t=NT)
        out_v = out.rearrange("(p t) f -> p t f", t=NT)
        p_v = p_table.rearrange("(p t) h -> p t h", t=NT)
        q_v = q_table[0:NODES, :].rearrange("(p t) h -> p t h", t=NT)

        def columns_of(table, t):
            return table[:, QE * t:QE * (t + 1)].rearrange("e (q c) -> e c q", c=4)

        def tile_of(b):
            return b[:, :].rearrange("e (c q) -> e c q", c=4)

        def parts(rows):
            return [(m, 4 * m, min(4, rows - 4 * m)) for m in range(-(-rows // 4))]

        def rounds(eng, first, last, step):
            whole = (last - first) // RING
            with eng.Fori(0, whole) as i:
                for j in range(first, first + RING):
                    step(i * RING + j, j % RING, i + j // RING)
            for n in range(first + whole * RING, last):
                step(n, n % RING, n // RING)

        def chunks_of(n):
            return CHUNKS - 4 * n if isinstance(n, int) and n == QUADS - 1 else 4

        def if_one_window(eng, fast, general):
            eng.wait_ge(widest_done, 1)
            most_nodes = eng.value_load(widest[0:1, 0:1], min_val=0, max_val=NODES - 1)
            with eng.If(most_nodes < WIN):
                fast()
            with eng.Else():
                general()

        def window_start(eng, low_n, j):
            return nc.s_assert_within(eng.snap(low_n + j * WIN), 0, NODES - 1, skip_runtime_bounds_check_because=
                                      "the quad's windows start at or below its largest dst")

        def first_rows_in(eng):
            for k in range(RING):
                eng.wait_ge(gathered[k], 64)

        def items(eng, per_quad, per_window, after=None):
            count_items = eng.alloc_register("items")
            eng.reg_mov(count_items, 1)
            eng.wait_ge(windows_counted, 1)
            with eng.Fori(0, QUADS) as n:
                if per_quad:
                    per_quad(n)
                quad_windows = eng.value_load(windows_of[0:1, bass.ds(n, 1)], min_val=0, max_val=MOST)
                with eng.Fori(0, quad_windows) as j:
                    per_window(n, j, eng.snap(count_items))
                    eng.reg_add(count_items, count_items, 1)
                if after:
                    after(n)
            return eng.snap(count_items)

        def done(n):
            return n + (1 + RING)

        @block.sync
        def _(sp):
            def load_edges(what, to, loaded):
                at = (QT - 1) * 128 * QE
                rows = FULL - (QT - 1) * 128
                sp.dma_start(to[:, 0:QT - 1, :],
                             what[0:at].rearrange("(t p e) -> p t e", p=128, e=QE)).then_inc(loaded, 16)
                sp.dma_start(to[0:rows, QT - 1, :],
                             what[at:at + rows * QE].rearrange("(p e) -> p e", e=QE)).then_inc(loaded, 16)
                sp.dma_start(to[rows:rows + 1, QT - 1, 0:REST],
                             what[FULL * QE:EDGES].rearrange("(p e) -> p e", p=1)).then_inc(loaded, 16)

            for n in range(LOADS):
                s = slice(n * XT, (n + 1) * XT)
                sp.dma_start(xs[0:SPLIT, s, :], x_v[0:SPLIT, s, :]).then_inc(x_in[n], 16)
                sp.dma_start(xs[SPLIT:NP, s, :], x_v[SPLIT:NP, s, :]).then_inc(x_in[n], 16)
                if n == 0:
                    sp.wait_ge(pads, 1)
                    load_edges(src, src_i, src_in)
            sp.wait_ge(pads, 2)
            load_edges(dst, dst_i, dst_in)

            sp.wait_ge(zeroed, 1)
            sp.dma_start(q_table[NODES:NODES + WIN, :], zeros[0:WIN, :]).then_inc(q_pad, 16)
            for table, staged, stored, first in ((p_v, p_staged, p_out, 0), (q_v, q_staged, q_out, GROUPS)):
                for n in range(GROUPS):
                    k = (first + n) % STAGES
                    s = slice(n * GT, (n + 1) * GT)
                    sp.wait_ge(staged, 3 * (n + 1))
                    sp.dma_start(table[0:SPLIT, s, :], stage[k][0:SPLIT]).then_inc(stored[k], 16)
                    sp.dma_start(table[SPLIT:NP, s, :], stage[k][SPLIT:NP]).then_inc(stored[k], 16)
            for k in range(STAGES):
                sp.wait_ge(q_out[k], q_all_out[k])
            sp.dma_start(count.rearrange("o (p c) -> o p c", p=128), zeros[:, 0:ACOLS // 128]).then_inc(count_zero, 16)
            sp.wait_ge(q_pad, 16)
            sp.wait_ge(windows, 1)

            def load_window(n, k, use):
                sp.wait_ge(zq_done, done(n - RING))
                at = sp.value_load(base_i[0:1, bass.ds(n, 1)], min_val=0, max_val=NODES - 1)
                sp.dma_start(qw[:, k, :], q_table[bass.ds(at, WIN), :]).then_inc(window_in[k], 16)

            def fast():
                rounds(sp, 0, QUADS, load_window)
                sp.wait_ge(c_done, done(QUADS - 1))

            def general():
                def load_general(n, j, m):
                    low_n = sp.value_load(base_i[0:1, bass.ds(n, 1)], min_val=0, max_val=NODES - 1)
                    at = window_start(sp, low_n, j)
                    sp.wait_ge(item_done, m)
                    sp.dma_start(qw[:, 0, :], q_table[bass.ds(at, WIN), :]).then_inc(w_loaded, 16)

                items(sp, None, load_general)
                sp.wait_ge(all_added, 1)

            if_one_window(sp, fast, general)

            sp.dma_start(count_t[:, :], count[:, 0:NODES].rearrange("o (p t) -> o p t", t=NT)).then_inc(count_in, 16)

            for b, end in zip(STORES, STORES[1:]):
                s = slice(BT * b, BT * end)
                sp.wait_ge(res_done, BT * end)
                sp.dma_start(out_v[0:SPLIT, s, :], xs[0:SPLIT, s, :]).then_inc(out_done, 16)
                sp.dma_start(out_v[SPLIT:NP, s, :], xs[SPLIT:NP, s, :]).then_inc(out_done, 16)
            sp.wait_ge(out_done, 32 * (len(STORES) - 1))

        @block.gpsimd
        def _(pool):
            nc.gpsimd.memset(src_i[:, QT - 1, :], 0).then_inc(pads, 1)
            nc.gpsimd.memset(dst_i[:, QT - 1, :], PAD).then_inc(pads, 1)
            nc.gpsimd.memset(w1[:, :, :, :], 0.0).then_inc(w1_zero, 1)
            nc.gpsimd.memset(w2[:, :], 0.0).then_inc(w1_zero, 1)
            nc.gpsimd.memset(eps[:, :], EPS).then_inc(eps_there, 1)
            nc.gpsimd.memset(ident[:, :], 0.0).then_inc(consts, 1)
            pool.wait_ge(consts, 1)
            nc.gpsimd.affine_select(out=ident[:, :], in_=ident[:, :], compare_op=ALU.not_equal, fill=1.0,
                                    base=0, pattern=[[-1, 128]], channel_multiplier=1).then_inc(consts, 1)
            pool.wait_ge(consts, 2)
            nc.gpsimd.tensor_copy(ident16[:, :], ident[:, :]).then_inc(consts, 1)
            nc.gpsimd.iota(columns[:, :], pattern=[[1, WIN]], base=0, channel_multiplier=0,
                           allow_small_or_imprecise_dtypes=True).then_inc(consts, 1)
            nc.gpsimd.memset(ones16[:, :], 1.0).then_inc(consts, 1)
            nc.gpsimd.memset(zeros[:, :], 0.0).then_inc(zeroed, 1)

            nc.gpsimd.iota(shift[:, :], pattern=[[WIN, MOST]], base=0, channel_multiplier=0,
                           allow_small_or_imprecise_dtypes=True).then_inc(consts, 1)

            def centre(n):
                s = slice(n * GT, (n + 1) * GT)
                pool.wait_ge(mean_done, n + 1)
                if n >= CENTRED:
                    pool.wait_ge(h_done, n - CENTRED + 1)
                nc.gpsimd.tensor_tensor(centred[n % CENTRED], xs[:, s, :],
                                        mean[:, s].unsqueeze(2).to_broadcast([NP, GT, FEAT]),
                                        ALU.subtract).then_inc(centred_done, 1)

            def square(n):
                pool.wait_ge(centred_done, n + 1)
                if n >= 2:
                    pool.wait_ge(ss_done, n - 1)
                c = centred[n % CENTRED]
                nc.gpsimd.tensor_tensor(squares[:, n % 2], c, c, ALU.mult).then_inc(sq_done, 1)

            for n in range(GROUPS):
                centre(n)
                square(n)
            for k in range(1, STAGES):
                pool.wait_ge(p_out[k], all_out[k])

            def gather(n, k, use):
                ready = pool.to_reg(n + 1)
                pool.wait_ge(p_out[0], all_out[0])
                pool.wait_ge(idx_ready, ready)
                for j in range(chunks_of(n)):
                    nc.gpsimd.indirect_dma_start(
                        out=g[:, k, j * HID:(j + 1) * HID], out_offset=None, in_=p_table,
                        in_offset=bass.IndirectOffsetOnAxis(ap=idx[:, k, j:j + 1], axis=0)).then_inc(gathered[k], 16)

            def general():
                first_rows_in(pool)

                def gather_general(n):
                    ready = pool.to_reg(n + 1)
                    pool.wait_ge(p_out[0], all_out[0])
                    pool.wait_ge(rows_ready, ready)
                    for j in range(4):
                        nc.gpsimd.indirect_dma_start(
                            out=g[:, 0, j * HID:(j + 1) * HID], out_offset=None, in_=p_table,
                            in_offset=bass.IndirectOffsetOnAxis(ap=idx[:, 0, j:j + 1], axis=0)).then_inc(rows_in, 16)

                with pool.Fori(0, QUADS) as n:
                    gather_general(n)

            for n in range(RING):
                gather(n, n, 0)
            if_one_window(pool, lambda: rounds(pool, RING, QUADS, gather), general)

            pool.wait_ge(b2_in, 16)
            pool.wait_ge(any_done, 1)
            for b in range(BATCHES):
                s = slice(BT * b, BT * (b + 1))
                if b < POOL_BATCHES:
                    nc.gpsimd.tensor_tensor(b2_any[:, b], any_edge[:, s].unsqueeze(2).to_broadcast([NP, BT, FEAT]),
                                            b2_all[:, :].unsqueeze(1).to_broadcast([NP, BT, FEAT]),
                                            ALU.mult).then_inc(b2_first, 1)
                    pool.wait_ge(b2_first, b + 1)
                else:
                    pool.wait_ge(b2_scaled, BT * (b - POOL_BATCHES + 1))
                nc.gpsimd.tensor_tensor(xs[:, s, :], xs[:, s, :], b2_any[:, b % PLACES], ALU.add).then_inc(b2_added, 1)

        @block.scalar
        def _(act):
            nc.scalar.preload_act_table(ACT.Sqrt)
            act.dma_start(b1_all[:, :], b1.rearrange("(o h) -> o h", o=1).to_broadcast([NP, HID])).then_inc(b1_in, 16)
            act.dma_start(b2_all[:, :], b2.rearrange("(o f) -> o f", o=1).to_broadcast([NP, FEAT])).then_inc(b2_in, 16)
            act.wait_ge(w1_zero, 2)
            for half in (0, 1):
                act.dma_start(w1[FEAT * half:FEAT * (half + 1), half, :, :],
                              W1.rearrange("(a f) h -> f a h", a=2)).then_inc(w_in, 16)
            act.dma_start(w2[:, 0:FEAT], W2).then_inc(w2_in, 16)

            def root_of(n):
                act.wait_ge(ss_done, n + 1)
                nc.scalar.activation(stats[:, n % 2, 1, :], stats[:, n % 2, 0, :], ACT.Sqrt, bias=eps[:, :],
                                     scale=1.0 / FEAT).then_inc(std_done, 1)

            def ht_of(n):
                act.wait_ge(ht_psum, n + 1)
                nc.scalar.copy(ht[n][:, 0:4, :],
                               h_bank[0][:, 0:4 * NP].rearrange("p (i n) -> p i n", i=4)).then_inc(ht_done, 1)
                nc.scalar.copy(ht[n][:, 4, :], h_bank[1][:, 0:NP]).then_inc(ht_done, 1)

            def p_of(n):
                act.wait_ge(p_psum, n + 1)
                if n >= STAGES:
                    act.wait_ge(p_out[n % STAGES], 32 * (n // STAGES))
                for m, t, w in parts(GT):
                    nc.scalar.copy(stage[n % STAGES][:, t:t + w, :],
                                   rows_bank[n % 2][m][0:NP, 0:HID * w].rearrange("p (t h) -> p t h", t=w))\
                        .then_inc(p_staged, 1)

            act.wait_ge(eps_there, 1)
            root_of(0)

            for t in range(QT):
                act.wait_ge(src_psum, t + 1)
                nc.scalar.copy(columns_of(src_e, t), tile_of(bank[2 + t])).then_inc(src_table, 1)

            for n in range(GROUPS + 2):
                if 1 <= n < GROUPS:
                    root_of(n)
                if 1 <= n <= GROUPS:
                    ht_of(n - 1)
                if n >= 2:
                    p_of(n - 2)
            act.wait_ge(src_table, QT)
            for n in range(RING):
                nc.scalar.copy(idx[:, n, :], src_e[:, n * 4:n * 4 + 4]).then_inc(idx_ready, 1)

            act.wait_ge(base_psum, 1)
            nc.scalar.copy(base[:, :], bank[0][:, :]).then_inc(base_done, 1)

            act.wait_ge(dst_table, QT)
            act.wait_ge(zeroed, 1)
            nc.scalar.copy(acc[:, :], zeros[:, 0:1].to_broadcast([128, ACOLS])).then_inc(u_zero, 1)

            for credit in (member16_done, spread_done, r_done):
                act.sem_inc(credit, RING)

            def indices_of(n, k):
                act.wait_ge(z_done, done(n - RING))
                nc.scalar.copy(idx[:, k, :], src_e[:, bass.ds(n * 4, 4)]).then_inc(idx_ready, 1)

            def spread_of(n, k, use):
                act.wait_ge(t_psum, done(n))
                act.wait_ge(zq_done, done(n - 2))
                w = 128 * chunks_of(n)
                nc.scalar.copy(spread[:, k % 2, :, :].rearrange("p c e -> p (c e)")[:, 0:w],
                               t_bank[k % 2][:, 0:w]).then_inc(spread_done, 1)

            def relu(n, k, use):
                w = HID * chunks_of(n)
                act.wait_ge(z_done, done(n))
                act.wait_ge(u_psum, done(n - 2))
                nc.scalar.activation(r[:, k % 2, 0:w], z[:, k % 2, 0:w], ACT.Relu).then_inc(r_done, 1)

            def member16_of(n, k, use):
                act.wait_ge(member_done, done(n))
                act.wait_ge(u_psum, done(n - MEMBERS))
                c = chunks_of(n)
                nc.scalar.copy(member16[:, k % MEMBERS, 0:c, :], member[:, k % MEMBERS, 0:c, :]).then_inc(member16_done, 1)

            def quads(n, k, use):
                here = isinstance(n, int)
                if not here or RING <= n + LEAD < QUADS:
                    indices_of(n + LEAD, (k + LEAD) % RING)
                if here and n == 2:
                    act.wait_ge(q_pad, 16)
                    act.wait_ge(count_zero, 16)
                if not here or 1 <= n <= QUADS:
                    spread_of(n - 1, (k - 1) % RING, 0)
                if not here or 2 <= n <= QUADS + 1:
                    relu(n - 2, (k - 2) % RING, 0)
                if not here or n < QUADS:
                    member16_of(n, k, 0)

            def fast():
                for n in range(LAG):
                    quads(n, n, 0)
                rounds(act, LAG, QUADS - LEAD, quads)
                for n in range(QUADS - LEAD, QUADS + LAG):
                    quads(n, n % RING, n // RING)

            def general():
                first_rows_in(act)

                def indices_general(n):
                    act.wait_ge(rows_used, n + 1)
                    nc.scalar.copy(idx[:, 0, :], src_e[:, bass.ds(n * 4, 4)]).then_inc(rows_ready, 1)

                def window_general(n, j, m):
                    act.wait_ge(m_made, m)
                    nc.scalar.copy(member16[:, 0, :, :], member[:, 0, :, :]).then_inc(m_copied, 1)
                    act.wait_ge(m_turned, m)
                    nc.scalar.copy(spread[:, 0, :, :].rearrange("p c e -> p (c e)"), t_bank[0][:, 0:512])\
                        .then_inc(m_spread, 1)
                    act.wait_ge(z_made, m)
                    nc.scalar.activation(r[:, 0, :], z[:, 0, :], ACT.Relu).then_inc(r_made, 1)

                items(act, indices_general, window_general)

            if_one_window(act, fast, general)

            act.wait_ge(b2_in, 16)
            act.wait_ge(any_done, 1)
            for t in range(BT * POOL_BATCHES, NT):
                if t % BT == 0 and t >= BT * PLACES:
                    act.wait_ge(b2_added, t // BT - PLACES + 1)
                nc.scalar.activation(b2_any[:, t // BT % PLACES, t % BT, :], b2_all[:, :], ACT.Copy,
                                     scale=any_edge[:, t:t + 1]).then_inc(b2_scaled, 1)

        @block.vector
        def _(dve):
            def mean_of(n):
                s = slice(n * GT, (n + 1) * GT)
                dve.wait_ge(x_in[n * GT // XT], 32)
                nc.vector.tensor_reduce(total[:, s], xs[:, s, :], AX.X, ALU.add).then_inc(total_done, 1)
                dve.wait_ge(total_done, n + 1)
                nc.vector.tensor_scalar(mean[:, s], total[:, s], 1.0 / FEAT, None, ALU.mult).then_inc(mean_done, 1)

            def sum_squares(n):
                dve.wait_ge(sq_done, n + 1)
                nc.vector.tensor_reduce(stats[:, n % 2, 0, :], squares[:, n % 2], AX.X, ALU.add).then_inc(ss_done, 1)

            def normalise(n):
                std, rstd = stats[:, n % 2, 1, :], stats[:, n % 2, 2, :]
                dve.wait_ge(std_done, n + 1)
                nc.vector.reciprocal(rstd, std).then_inc(rstd_done, 1)
                dve.wait_ge(rstd_done, n + 1)
                if n >= HS:
                    dve.wait_ge(ht_psum, n - HS + 1)
                nc.vector.scalar_tensor_tensor(hs[n % HS], centred[n % CENTRED], 0.0,
                                               rstd.unsqueeze(2).to_broadcast([NP, GT, FEAT]),
                                               ALU.max, ALU.mult).then_inc(h_done, 1)

            def rel_of(t):
                dve.wait_ge(dst_psum, t + 1)
                w = base[:, 128 * t:128 * (t + 1)].rearrange("e (o q) -> e o q", o=1)
                nc.vector.tensor_tensor(columns_of(rel_e, t), tile_of(bank[t % 2]), w.to_broadcast([128, 4, 128]),
                                        ALU.subtract).then_inc(dst_table, 1)

            def smallest():
                dve.wait_ge(dst_in, 48)
                nc.vector.tensor_copy(dst_f, dst_i).then_inc(dst_cast, 1)
                nc.vector.tensor_reduce(low[:, :], dst_i, AX.X, ALU.min).then_inc(low_done, 1)

            def largest():
                dve.wait_ge(dst_cast, 1)
                nc.vector.tensor_reduce(high[:, 0:QT - 1], dst_f[:, 0:QT - 1, :], AX.X, ALU.max)
                nc.vector.scalar_tensor_tensor(real[:, :], dst_f[:, QT - 1, :], float(PAD), dst_f[:, QT - 1, :],
                                               ALU.is_lt, ALU.mult).then_inc(real_done, 1)

            def spans():
                dve.wait_ge(real_done, 1)
                nc.vector.tensor_reduce(high[:, QT - 1:QT], real[:, :], AX.X, ALU.max).then_inc(high_done, 1)
                dve.wait_ge(high_done, 1)
                nc.vector.tensor_tensor(span[:, :], high[:, :], low[:, :], ALU.subtract).then_inc(span_done, 1)

            mean_of(0)
            mean_of(1)
            dve.wait_ge(src_in, 48)
            nc.vector.tensor_copy(src_f, src_i).then_inc(src_cast, 1)
            for n in range(GROUPS + 1):
                if n < GROUPS:
                    sum_squares(n)
                if n + 2 < GROUPS:
                    mean_of(n + 2)
                if n < EARLY:
                    normalise(n)
                if n > EARLY:
                    normalise(n - 1)
            smallest()
            largest()
            spans()

            dve.wait_ge(span_psum, 1)
            nc.vector.tensor_copy(spans_i[:, :], bank[1][0:1, :]).then_inc(span_done_i, 1)
            dve.wait_ge(span_done_i, 1)
            nc.vector.tensor_reduce(widest[:, :], spans_i[:, 0:QUADS], AX.X, ALU.max).then_inc(widest_done, 1)
            dve.wait_ge(base_done, 1)
            nc.vector.tensor_copy(base_i[:, :], base[0:1, :]).then_inc(windows, 1)

            dve.wait_ge(b1_in, 16)
            for n in range(GROUPS):
                dve.wait_ge(q_psum, n + 1)
                k = (GROUPS + n) % STAGES
                if n < STAGES:
                    dve.wait_ge(p_out[k], all_out[k])
                else:
                    dve.wait_ge(q_out[k], 32 * (n // STAGES))
                for m, t, w in parts(GT):
                    nc.vector.tensor_tensor(stage[k][:, t:t + w, :],
                                            rows_bank[n % 2][m][0:NP, 0:HID * w].rearrange("p (t h) -> p t h", t=w),
                                            b1_all[:, :].unsqueeze(1).to_broadcast([NP, w, HID]),
                                            ALU.add).then_inc(q_staged, 1)
                if n < QT:
                    rel_of(n)

            for credit in (member_done, z_done, u_done, c_done):
                dve.sem_inc(credit, RING)

            def members_of(n, k, use):
                dve.wait_ge(u_psum, done(n - MEMBERS))
                dve.wait_ge(member16_done, done(n - MEMBERS))
                for j in range(chunks_of(n)):
                    last = nc.vector.tensor_scalar(member[:, k % MEMBERS, j, :], columns[:, :],
                                                   rel_e[:, bass.ds(n * 4 + j, 1)], None, ALU.is_equal)
                last.then_inc(member_done, 1)

            def add_rows(n, k, use):
                w = HID * chunks_of(n)
                dve.wait_ge(zq_done, done(n))
                dve.wait_ge(gathered[k], use * 64 + 16 * chunks_of(n))
                dve.wait_ge(r_done, done(n - 2))
                nc.vector.tensor_tensor(z[:, k % 2, 0:w], z_bank[k % 2][:, 0:w], g[:, k, 0:w],
                                        ALU.add).then_inc(z_done, 1)

            def window_of(n, of):
                at = dve.value_load(base_i[0:1, bass.ds(n, 1)], min_val=0, max_val=NODES - 1)
                return of[:, bass.ds(at, WIN)]

            def add_counts(n, k, use):
                c = window_of(n, count)
                dve.wait_ge(c_psum, done(n))
                dve.wait_ge(c_done, done(n - 1))
                nc.vector.tensor_tensor(c, c, c_bank[k % 2][0:1, 0:WIN], ALU.add).then_inc(c_done, 1)

            def add_sums(n, k, use):
                u = window_of(n, acc)
                dve.wait_ge(u_psum, done(n))
                dve.wait_ge(u_done, done(n - 1))
                nc.vector.tensor_tensor(u, u, u_bank[k % 2][:, 0:WIN], ALU.add).then_inc(u_done, 1)

            def scales():
                dve.wait_ge(count_in, 16)
                nc.vector.tensor_scalar(any_edge[:, :], count_t[:, :], 1.0, None, ALU.min).then_inc(any_done, 1)
                nc.vector.tensor_scalar(most[:, :], count_t[:, :], 1.0, None, ALU.max).then_inc(most_done, 1)
                dve.wait_ge(most_done, 1)
                nc.vector.reciprocal(inverse[:, :], most[:, :]).then_inc(inverse_done, 1)

            def quads(n, k, use):
                here = isinstance(n, int)
                if not here or n < QUADS:
                    members_of(n, k, 0)
                if here and n == 1:
                    dve.wait_ge(count_zero, 16)
                if not here or 1 <= n <= QUADS:
                    add_counts(n - 1, (k - 1) % RING, 0)
                if not here or 2 <= n <= QUADS + 1:
                    add_rows(n - 2, (k - 2) % RING, use - (1 if k < 2 else 0))
                if here and n == QUADS + 1:
                    scales()
                if here and n == 3:
                    dve.wait_ge(u_zero, 1)
                if not here or n >= 3:
                    add_sums(n - 3, (k - 3) % RING, 0)

            def fast():
                for n in range(LAG):
                    quads(n, n, 0)
                rounds(dve, LAG, QUADS - LEAD, quads)
                for n in range(QUADS - LEAD, QUADS + LAG):
                    quads(n, n % RING, n // RING)

            def general():
                first_rows_in(dve)
                dve.wait_ge(span_done_i, 1)
                nc.vector.tensor_scalar(windows_of[:, :], spans_i[:, :], WIN.bit_length() - 1, None,
                                        ALU.arith_shift_right).then_inc(windows_shifted, 1)
                dve.wait_ge(windows_shifted, 1)
                nc.vector.tensor_scalar(windows_of[:, :], windows_of[:, :], 1, None, ALU.add)\
                    .then_inc(windows_counted, 1)
                dve.wait_ge(count_zero, 16)
                dve.wait_ge(u_zero, 1)
                dve.sem_inc(item_done, 1)
                dve.sem_inc(rows_used, 1)

                def window_general(n, j, m):
                    low_n = dve.value_load(base_i[0:1, bass.ds(n, 1)], min_val=0, max_val=NODES - 1)
                    at = window_start(dve, low_n, j)
                    u, c = acc[:, bass.ds(at, WIN)], count[:, bass.ds(at, WIN)]
                    gathers = dve.to_reg((n + 1) * 64)
                    dve.wait_ge(item_done, m)
                    for k in range(4):
                        last = nc.vector.tensor_scalar(member[:, 0, k, :], columns[:, :], shift[:, bass.ds(j, 1)],
                                                       rel_e[:, bass.ds(n * 4 + k, 1)], ALU.add, ALU.is_equal)
                    last.then_inc(m_made, 1)
                    dve.wait_ge(q_spread, m)
                    dve.wait_ge(rows_in, gathers)
                    nc.vector.tensor_tensor(z[:, 0, :], z_bank[0][:, :], g[:, 0, :], ALU.add).then_inc(z_made, 1)
                    dve.wait_ge(u_made, m)
                    nc.vector.tensor_tensor(u, u, u_bank[0][:, 0:WIN], ALU.add).then_inc(u_added, 1)
                    dve.wait_ge(u_added, m)
                    nc.vector.tensor_tensor(c, c, c_bank[0][0:1, 0:WIN], ALU.add).then_inc(item_done, 1)

                def quad_done(n):
                    dve.sem_inc(rows_used, 1)

                dve.wait_ge(item_done, items(dve, None, window_general, quad_done))
                dve.sem_inc(all_added, 1)
                scales()

            if_one_window(dve, fast, general)

            dve.wait_ge(inverse_done, 1)
            for b in range(BATCHES):
                dve.wait_ge(o_psum, b + 1)
                dve.wait_ge(b2_added, b + 1)
                for t in range(BT * b, BT * (b + 1)):
                    nc.vector.scalar_tensor_tensor(xs[:, t, :], bank[b % 8][0:NP, 128 * (t % BT):128 * (t % BT) + FEAT],
                                                   inverse[:, t:t + 1], xs[:, t, :],
                                                   ALU.mult, ALU.add).then_inc(res_done, 1)

        @block.tensor
        def _(pe):
            def transposed(table, t, to, psum):
                for c in range(4):
                    last = nc.tensor.transpose(to[:, 128 * c:128 * (c + 1)], table[:, t, 128 * c:128 * (c + 1)],
                                               ident[:, :])
                last.then_inc(psum, 1)

            pe.wait_ge(consts, 5)
            pe.wait_ge(src_cast, 1)
            for t in range(QT):
                transposed(src_f, t, bank[2 + t], src_psum)

            def transpose_h(n):
                pe.wait_ge(h_done, n + 1)
                if n:
                    pe.wait_ge(ht_done, 2 * n)
                for i in range(GT // 2):
                    last = nc.tensor.transpose(h_bank[i // 4][:, NP * (i % 4):NP * (i % 4 + 1)],
                                               hs[n % HS][:, 2 * i:2 * i + 2, :].rearrange("p t f -> p (t f)"),
                                               ident[0:NP, 0:NP])
                last.then_inc(ht_psum, 1)

            def products(n, half, psum):
                for t in range(GT):
                    last = nc.tensor.matmul(rows_bank[n % 2][t // 4][0:NP, HID * (t % 4):HID * (t % 4 + 1)],
                                            ht[n][:, t // 2, :], w1[:, t % 2, half, :], start=True, stop=True)
                last.then_inc(psum, 1)

            def spans_and_starts():
                pe.wait_ge(span_done, 1)
                for t in range(QT):
                    last = nc.tensor.matmul(bank[1][0:1, 128 * t:128 * (t + 1)], span[:, t:t + 1], ident[:, :],
                                            start=True, stop=True)
                last.then_inc(span_psum, 1)
                for t in range(QT):
                    last = nc.tensor.matmul(bank[0][:, 128 * t:128 * (t + 1)], low[:, t:t + 1].to_broadcast([128, 128]),
                                            ident[:, :], start=True, stop=True)
                last.then_inc(base_psum, 1)

            pe.wait_ge(w_in, 32)
            for n in range(GROUPS + 1):
                if 1 != n < GROUPS:
                    transpose_h(n)
                if n:
                    if n == 1:
                        pe.wait_ge(src_table, QT)
                    pe.wait_ge(ht_done, 2 * n)
                    if n > 2:
                        pe.wait_ge(p_staged, 3 * (n - 2))
                    products(n - 1, 0, p_psum)
                if n == GROUPS:
                    spans_and_starts()
                if n == 1:
                    transpose_h(1)
            for n in range(GROUPS):
                if n < 2:
                    pe.wait_ge(p_staged, 3 * (GROUPS - 1 + n))
                else:
                    pe.wait_ge(q_staged, 3 * (n - 1))
                products(n, 1, q_psum)
                if n < QT:
                    if n < 2:
                        pe.wait_ge(*((base_done, 1), (span_done_i, 1))[n])
                    else:
                        pe.wait_ge(dst_table, n - 1)
                    transposed(dst_f, n, bank[n % 2], dst_psum)

            pe.wait_ge(q_staged, 3 * GROUPS)
            for credit in (t_psum, c_psum, zq_done, u_psum):
                pe.sem_inc(credit, RING)

            def spread_q(n, k, use):
                pe.wait_ge(spread_done, done(n))
                pe.wait_ge(window_in[k], use * 16 + 16)
                pe.wait_ge(z_done, done(n - 2))
                for j in range(chunks_of(n)):
                    last = nc.tensor.matmul(z_bank[k % 2][:, HID * j:HID * (j + 1)], spread[:, k % 2, j, :],
                                            qw[:, k, :], start=True, stop=True)
                last.then_inc(zq_done, 1)

            def sum_edges(n, k, use):
                pe.wait_ge(r_done, done(n))
                pe.wait_ge(u_done, done(n - 2))
                sums = u_bank[k % 2]
                chunks = chunks_of(n)
                for c in range(chunks):
                    last = nc.tensor.matmul(sums[:, 0:WIN], r[:, k % 2, HID * c:HID * (c + 1)],
                                            member[:, k % MEMBERS, c, :], start=c == 0, stop=c == chunks - 1)
                last.then_inc(u_psum, 1)

            def transpose_members(n, k, use):
                pe.wait_ge(member16_done, done(n))
                pe.wait_ge(spread_done, done(n - 2))
                for c in range(chunks_of(n)):
                    last = nc.tensor.transpose(t_bank[k % 2][:, 128 * c:128 * (c + 1)], member16[:, k % MEMBERS, c, :],
                                               ident16[:, :])
                last.then_inc(t_psum, 1)
                pe.wait_ge(c_done, done(n - 2))
                for c in range(chunks_of(n)):
                    last = nc.tensor.matmul(c_bank[k % 2][0:1, 0:WIN], ones16[:, :], member16[:, k % MEMBERS, c, :],
                                            start=c == 0, stop=c == chunks_of(n) - 1)
                last.then_inc(c_psum, 1)

            def quads(n, k, use):
                here = isinstance(n, int)
                if not here or 1 <= n <= QUADS:
                    spread_q(n - 1, (k - 1) % RING, use - (0 if k else 1))
                if not here or 2 <= n <= QUADS + 1:
                    sum_edges(n - 2, (k - 2) % RING, 0)
                if not here or n < QUADS:
                    transpose_members(n, k, 0)

            def fast():
                for n in range(LAG):
                    quads(n, n, 0)
                rounds(pe, LAG, QUADS - LEAD, quads)
                for n in range(QUADS - LEAD, QUADS + LAG):
                    quads(n, n % RING, n // RING)
                pe.wait_ge(u_done, done(QUADS - 1))
                pe.wait_ge(c_done, done(QUADS - 1))

            def general():
                def window_general(n, j, m):
                    loads = pe.to_reg(m * 16)
                    pe.wait_ge(m_copied, m)
                    for c in range(4):
                        last = nc.tensor.transpose(t_bank[0][:, 128 * c:128 * (c + 1)], member16[:, 0, c, :],
                                                   ident16[:, :])
                    last.then_inc(m_turned, 1)
                    pe.wait_ge(m_spread, m)
                    pe.wait_ge(w_loaded, loads)
                    for c in range(4):
                        last = nc.tensor.matmul(z_bank[0][:, HID * c:HID * (c + 1)], spread[:, 0, c, :], qw[:, 0, :],
                                                start=True, stop=True)
                    last.then_inc(q_spread, 1)
                    pe.wait_ge(r_made, m)
                    for c in range(4):
                        nc.tensor.matmul(u_bank[0][:, 0:WIN], r[:, 0, HID * c:HID * (c + 1)], member[:, 0, c, :],
                                         start=c == 0, stop=c == 3)
                    for c in range(4):
                        last = nc.tensor.matmul(c_bank[0][0:1, 0:WIN], ones16[:, :], member16[:, 0, c, :],
                                                start=c == 0, stop=c == 3)
                    last.then_inc(u_made, 1)

                items(pe, None, window_general)
                pe.wait_ge(all_added, 1)

            if_one_window(pe, fast, general)

            pe.wait_ge(w2_in, 16)
            for b in range(BATCHES):
                if b >= 8:
                    pe.wait_ge(res_done, BT * (b - 7))
                for t in range(BT):
                    node = slice(BT * b + t, BT * b + t + (NP - 1) * NT + 1, NT)
                    last = nc.tensor.matmul(bank[b % 8][0:NP, 128 * t:128 * (t + 1)], acc[:, node], w2[:, :],
                                            start=True, stop=True)
                last.then_inc(o_psum, 1)


_INS = ["x", "src", "dst", "L0_gnn_W1", "L0_gnn_b1", "L0_gnn_W2", "L0_gnn_b2"]


def kernel(**inputs):
    import numpy as _np
    import concourse.bacc as _bacc
    from concourse import mybir as _mybir
    from concourse.bass_utils import run_bass_kernel_spmd as _run

    nc = _bacc.Bacc("TRN2", target_bir_lowering=False, num_devices=1)
    arrays, args = {}, []
    for name in _INS:
        a = _np.ascontiguousarray(inputs[name])
        arrays[f"in_{name}_dram"] = a
        args.append(nc.dram_tensor(f"in_{name}_dram", a.shape, _mybir.dt.from_np(a.dtype), kind="ExternalInput").ap())
    out = nc.dram_tensor("out_0_dram", [NODES, FEAT], F32, kind="ExternalOutput").ap()
    gnn_kernel(nc, *args, out)
    r = _run(nc, [arrays], core_ids=[0])
    return r.results[0]["out_0_dram"]
```

```python
from contextlib import ExitStack

import concourse.bass as bass
from concourse import mybir

F32 = mybir.dt.float32
BF16 = mybir.dt.bfloat16
I32 = mybir.dt.int32
ALU = mybir.AluOpType
ACT = mybir.ActivationFunctionType
AX = mybir.AxisListType

NODES, FEAT, HID, EDGES = 12500, 64, 128, 200000
EPS = 1e-5

NP = 125
NT = NODES // NP
GT = 10
GROUPS = NT // GT
SPLIT = 112
XT = 20
LOADS = NT // XT
GC = GT * FEAT

WIN = 128
QE = 512
QUADS = -(-EDGES // QE)
FULL = EDGES // QE
REST = EDGES - FULL * QE
CHUNKS = -(-EDGES // 128)
QT = -(-QUADS // 128)
RING = 12
PAD = 65535
MOST = NODES // WIN + 2
ACOLS = 12800
LEAD = 9
MEMBERS = 4
BT = 4
BATCHES = NT // BT
STORES = (0, 6, 12, 18, 23, BATCHES)
SHARED = tuple(range(1, 22, 2))
EARLY = 4
LAG = 4
CENTRED, HS, STAGES = 4, 3, 3


def gnn_kernel(nc, x, src, dst, W1, b1, W2, b2, out):
    p_table = nc.dram_tensor("p_table", [NODES, HID], F32).ap()
    q_table = nc.dram_tensor("q_table", [NODES + WIN, HID], F32).ap()

    ctx = ExitStack()
    with ctx:
        def sb(name, shape, dt=F32):
            return ctx.enter_context(nc.sbuf_tensor(name, shape, dt))

        def sem(name):
            return ctx.enter_context(nc.semaphore(name))

        def sems(names):
            return [sem(n) for n in names.split()]

        ident = sb("ident", [128, 128])
        ident16 = sb("ident16", [128, 128], BF16)
        columns = sb("columns", [128, WIN])
        ones16 = sb("ones16", [128, 1], BF16)
        w1 = sb("w1", [128, 2, 2, HID])
        b1_all = sb("b1_all", [NP, HID])
        w2 = sb("w2", [HID, 128])
        b2_row = sb("b2_row", [1, 128])

        xs = sb("xs", [NP, NT, FEAT])
        area = sb("area", [128, ACOLS])
        count = area[0:1, :]

        def of_area(rows, at, k, cols, **dims):
            return area[0:rows, at + k * cols:at + (k + 1) * cols].rearrange("p (a b) -> p a b", **dims)

        hs = [of_area(NP, 0, k, GC, a=GT) for k in range(HS)]
        ht = [of_area(128, HS * GC, n, NP * GT // 2, a=GT // 2) for n in range(GROUPS)]
        stage = [of_area(NP, HS * GC + NT * NP // 2, k, GT * HID, a=GT) for k in range(STAGES)]
        mean = sb("mean", [NP, NT])
        total = sb("total", [NP, NT])
        stats = sb("stats", [NP, 2, 3, GT])
        eps = sb("eps", [NP, 1])

        acc = sb("acc", [128, ACOLS])
        NE = QT * QE
        src_i, dst_i, src_f, dst_f = (acc[:, k * NE:(k + 1) * NE] for k in range(4))
        src_i, dst_i = (a.bitcast(I32).rearrange("p (t e) -> p t e", t=QT) for a in (src_i, dst_i))
        src_f, dst_f = (a.rearrange("p (t e) -> p t e", t=QT) for a in (src_f, dst_f))
        low = sb("low", [128, QT])
        high = sb("high", [128, QT])
        span = sb("span", [128, QT])
        spans_i = sb("spans_i", [1, QT * 128], I32)
        widest = sb("widest", [1, 1], I32)
        shift = sb("shift", [128, MOST])
        base = sb("base", [128, QT * 128])
        base_i = sb("base_i", [1, QT * 128], I32)
        src_e = sb("src_e", [128, QT * QE], I32)
        rel_e = sb("rel_e", [128, QT * QE])

        idx = sb("idx", [128, RING, 4], I32)
        g = sb("g", [128, RING, 4 * HID])
        qw = sb("qw", [WIN, RING, HID])
        rows = g[:, :, :].rearrange("p k c -> p (k c)")
        scaled = rows[0:NP, :].rearrange("p (b t f) -> p b t f", t=BT, f=FEAT)
        centred = [rows[0:NP, k * GC:(k + 1) * GC].rearrange("p (t f) -> p t f", t=GT) for k in range(CENTRED)]
        windows_of = g[0:1, 1, :].bitcast(I32)
        member = sb("member", [128, MEMBERS, 4, WIN])
        squares = member[0:NP, 0:3, :, :].rearrange("p k c w -> p (k c w)")[:, 0:2 * GC] \
            .rearrange("p (k t f) -> p k t f", k=2, t=GT)
        member16 = sb("member16", [128, MEMBERS, 4, WIN], BF16)
        spread = sb("spread", [WIN, 2, 4, 128])
        z = sb("z", [128, 2, 4 * HID])
        r = sb("r", [128, 2, 4 * HID])
        most, inverse = mean, total
        count_t = b1_all[:, 0:NT]
        sums_u = w1[:, 0, :, :]
        sums_c = spans_i.bitcast(F32)[:, :].rearrange("o (k w) -> o k w", w=WIN)
        zeros = spread[:, 1, 3, :]
        real = r[:, 0, :]

        bank = [ctx.enter_context(nc.psum_tensor(f"bank{i}", [128, 512], F32)) for i in range(8)]
        z_bank, u_bank, t_bank = bank[0:2], bank[2:4], [bank[4 + k][:, :].bitcast(BF16) for k in (0, 1)]
        c_bank = bank[6:8]
        h_bank, rows_bank = bank[0:2], [bank[2:5], bank[5:8]]

        rows_ready, rows_in, rows_used, w_loaded, m_made, m_copied, m_turned, m_spread, q_spread, z_made, r_made, \
            u_made, u_moved, c_moved, v_made, v_added, item_done, all_added = sems(
                "rows_ready rows_in rows_used w_loaded m_made m_copied m_turned m_spread q_spread z_made r_made "
                "u_made u_moved c_moved v_made v_added item_done all_added")
        high_done, real_done, span_done, span_psum, span_done_i, widest_done, windows_shifted, windows_counted = sems(
            "high_done real_done span_done span_psum span_done_i widest_done windows_shifted windows_counted")
        eps_there = sem("eps_there")

        consts, pads, w1_zero, zeroed, w_in, b1_in, w2_in, b2_in, src_in, dst_in, q_pad = sems(
            "consts pads w1_zero zeroed w_in b1_in w2_in b2_in src_in dst_in q_pad")
        dst_cast, src_cast, low_done, base_psum, base_done, windows, dst_psum, src_psum, dst_table, src_table = sems(
            "dst_cast src_cast low_done base_psum base_done windows dst_psum src_psum dst_table src_table")
        x_in = [sem(f"x_in{n}") for n in range(LOADS)]
        total_done, mean_done, centred_done, sq_done, ss_done, std_done, rstd_done, h_done = sems(
            "total_done mean_done centred_done sq_done ss_done std_done rstd_done h_done")
        ht_psum, ht_done, p_psum, q_psum, p_staged, q_staged = sems("ht_psum ht_done p_psum q_psum p_staged q_staged")
        p_out, q_out = ([sem(f"{table}_out{k}") for k in range(STAGES)] for table in "pq")
        all_out = [32 * len(range(k, GROUPS, STAGES)) for k in range(STAGES)]
        q_all_out = [32 * len(range((k - GROUPS) % STAGES, GROUPS, STAGES)) for k in range(STAGES)]
        v_zero, count_zero = sems("v_zero count_zero")
        idx_ready, member_done, member16_done, t_psum, c_psum, spread_done, zq_done, z_done, r_done, u_psum, v_psum, \
            v_done, c_done, c_copied, u_copied = sems(
                "idx_ready member_done member16_done t_psum c_psum spread_done zq_done z_done r_done u_psum v_psum "
                "v_done c_done c_copied u_copied")
        gathered = [sem(f"gathered{k}") for k in range(RING)]
        window_in = [sem(f"window_in{k}") for k in range(RING)]
        b2_zero, count_in, most_done, inverse_done, o_psum, scaled_done, added_done, res_done, out_done = sems(
            "b2_zero count_in most_done inverse_done o_psum scaled_done added_done res_done out_done")

        block = ctx.enter_context(nc.Block())

        x_v = x.rearrange("(p t) f -> p t f", t=NT)
        out_v = out.rearrange("(p t) f -> p t f", t=NT)
        p_v = p_table.rearrange("(p t) h -> p t h", t=NT)
        q_v = q_table[0:NODES, :].rearrange("(p t) h -> p t h", t=NT)

        def columns_of(table, t):
            return table[:, QE * t:QE * (t + 1)].rearrange("e (q c) -> e c q", c=4)

        def tile_of(b):
            return b[:, :].rearrange("e (c q) -> e c q", c=4)

        def parts(rows):
            return [(m, 4 * m, min(4, rows - 4 * m)) for m in range(-(-rows // 4))]

        def rounds(eng, first, last, step):
            whole = (last - first) // RING
            with eng.Fori(0, whole) as i:
                for j in range(first, first + RING):
                    step(i * RING + j, j % RING, i + j // RING)
            for n in range(first + whole * RING, last):
                step(n, n % RING, n // RING)

        def chunks_of(n):
            return CHUNKS - 4 * n if isinstance(n, int) and n == QUADS - 1 else 4

        def if_one_window(eng, fast, general):
            eng.wait_ge(widest_done, 1)
            most_nodes = eng.value_load(widest[0:1, 0:1], min_val=0, max_val=NODES - 1)
            with eng.If(most_nodes < WIN):
                fast()
            with eng.Else():
                general()

        def window_start(eng, low_n, j):
            return nc.s_assert_within(eng.snap(low_n + j * WIN), 0, NODES - 1, skip_runtime_bounds_check_because=
                                      "the quad's windows start at or below its largest dst")

        def first_rows_in(eng):
            for k in range(RING):
                eng.wait_ge(gathered[k], 64)

        def items(eng, per_quad, per_window, after=None):
            count_items = eng.alloc_register("items")
            eng.reg_mov(count_items, 1)
            eng.wait_ge(windows_counted, 1)
            with eng.Fori(0, QUADS) as n:
                if per_quad:
                    per_quad(n)
                quad_windows = eng.value_load(windows_of[0:1, bass.ds(n, 1)], min_val=0, max_val=MOST)
                with eng.Fori(0, quad_windows) as j:
                    per_window(n, j, eng.snap(count_items))
                    eng.reg_add(count_items, count_items, 1)
                if after:
                    after(n)
            return eng.snap(count_items)

        def shared(b):
            return sum(k < b for k in SHARED)

        def done(n):
            return n + (1 + RING)

        @block.sync
        def _(sp):
            def load_edges(what, to, loaded):
                at = (QT - 1) * 128 * QE
                rows = FULL - (QT - 1) * 128
                sp.dma_start(to[:, 0:QT - 1, :],
                             what[0:at].rearrange("(t p e) -> p t e", p=128, e=QE)).then_inc(loaded, 16)
                sp.dma_start(to[0:rows, QT - 1, :],
                             what[at:at + rows * QE].rearrange("(p e) -> p e", e=QE)).then_inc(loaded, 16)
                sp.dma_start(to[rows:rows + 1, QT - 1, 0:REST],
                             what[FULL * QE:EDGES].rearrange("(p e) -> p e", p=1)).then_inc(loaded, 16)

            for n in range(LOADS):
                s = slice(n * XT, (n + 1) * XT)
                sp.dma_start(xs[0:SPLIT, s, :], x_v[0:SPLIT, s, :]).then_inc(x_in[n], 16)
                sp.dma_start(xs[SPLIT:NP, s, :], x_v[SPLIT:NP, s, :]).then_inc(x_in[n], 16)
                if n == 0:
                    sp.wait_ge(pads, 1)
                    load_edges(src, src_i, src_in)
            sp.wait_ge(pads, 2)
            load_edges(dst, dst_i, dst_in)

            sp.wait_ge(zeroed, 1)
            sp.dma_start(q_table[NODES:NODES + WIN, :], zeros[0:WIN, :]).then_inc(q_pad, 16)
            for table, staged, stored, first in ((p_v, p_staged, p_out, 0), (q_v, q_staged, q_out, GROUPS)):
                for n in range(GROUPS):
                    k = (first + n) % STAGES
                    s = slice(n * GT, (n + 1) * GT)
                    sp.wait_ge(staged, 3 * (n + 1))
                    sp.dma_start(table[0:SPLIT, s, :], stage[k][0:SPLIT]).then_inc(stored[k], 16)
                    sp.dma_start(table[SPLIT:NP, s, :], stage[k][SPLIT:NP]).then_inc(stored[k], 16)
            for k in range(STAGES):
                sp.wait_ge(q_out[k], q_all_out[k])
            sp.dma_start(count.rearrange("o (p c) -> o p c", p=128), zeros[:, 0:ACOLS // 128]).then_inc(count_zero, 16)
            sp.wait_ge(q_pad, 16)
            sp.wait_ge(windows, 1)

            def load_window(n, k, use):
                sp.wait_ge(zq_done, done(n - RING))
                at = sp.value_load(base_i[0:1, bass.ds(n, 1)], min_val=0, max_val=NODES - 1)
                sp.dma_start(qw[:, k, :], q_table[bass.ds(at, WIN), :]).then_inc(window_in[k], 16)

            def fast():
                rounds(sp, 0, QUADS, load_window)
                sp.wait_ge(c_done, done(QUADS - 1))

            def general():
                def load_general(n, j, m):
                    low_n = sp.value_load(base_i[0:1, bass.ds(n, 1)], min_val=0, max_val=NODES - 1)
                    at = window_start(sp, low_n, j)
                    sp.wait_ge(item_done, m)
                    sp.dma_start(qw[:, 0, :], q_table[bass.ds(at, WIN), :]).then_inc(w_loaded, 16)

                items(sp, None, load_general)
                sp.wait_ge(all_added, 1)

            if_one_window(sp, fast, general)

            sp.dma_start(count_t[:, :], count[:, 0:NODES].rearrange("o (p t) -> o p t", t=NT)).then_inc(count_in, 16)

            for b, end in zip(STORES, STORES[1:]):
                s = slice(BT * b, BT * end)
                sp.wait_ge(res_done, BT * (end - shared(end)))
                sp.wait_ge(added_done, shared(end))
                sp.dma_start(out_v[0:SPLIT, s, :], xs[0:SPLIT, s, :]).then_inc(out_done, 16)
                sp.dma_start(out_v[SPLIT:NP, s, :], xs[SPLIT:NP, s, :]).then_inc(out_done, 16)
            sp.wait_ge(out_done, 32 * (len(STORES) - 1))

        @block.gpsimd
        def _(pool):
            nc.gpsimd.memset(src_i[:, QT - 1, :], 0).then_inc(pads, 1)
            nc.gpsimd.memset(dst_i[:, QT - 1, :], PAD).then_inc(pads, 1)
            nc.gpsimd.memset(w1[:, :, :, :], 0.0).then_inc(w1_zero, 1)
            nc.gpsimd.memset(w2[:, :], 0.0).then_inc(w1_zero, 1)
            nc.gpsimd.memset(b2_row[:, :], 0.0).then_inc(b2_zero, 1)
            nc.gpsimd.memset(eps[:, :], EPS).then_inc(eps_there, 1)
            nc.gpsimd.memset(ident[:, :], 0.0).then_inc(consts, 1)
            pool.wait_ge(consts, 1)
            nc.gpsimd.affine_select(out=ident[:, :], in_=ident[:, :], compare_op=ALU.not_equal, fill=1.0,
                                    base=0, pattern=[[-1, 128]], channel_multiplier=1).then_inc(consts, 1)
            pool.wait_ge(consts, 2)
            nc.gpsimd.tensor_copy(ident16[:, :], ident[:, :]).then_inc(consts, 1)
            nc.gpsimd.iota(columns[:, :], pattern=[[1, WIN]], base=0, channel_multiplier=0,
                           allow_small_or_imprecise_dtypes=True).then_inc(consts, 1)
            nc.gpsimd.memset(ones16[:, :], 1.0).then_inc(consts, 1)
            nc.gpsimd.memset(zeros[:, :], 0.0).then_inc(zeroed, 1)

            nc.gpsimd.iota(shift[:, :], pattern=[[WIN, MOST]], base=0, channel_multiplier=0,
                           allow_small_or_imprecise_dtypes=True).then_inc(consts, 1)

            def centre(n):
                s = slice(n * GT, (n + 1) * GT)
                pool.wait_ge(mean_done, n + 1)
                if n >= CENTRED:
                    pool.wait_ge(h_done, n - CENTRED + 1)
                nc.gpsimd.tensor_tensor(centred[n % CENTRED], xs[:, s, :],
                                        mean[:, s].unsqueeze(2).to_broadcast([NP, GT, FEAT]),
                                        ALU.subtract).then_inc(centred_done, 1)

            def square(n):
                pool.wait_ge(centred_done, n + 1)
                if n >= 2:
                    pool.wait_ge(ss_done, n - 1)
                c = centred[n % CENTRED]
                nc.gpsimd.tensor_tensor(squares[:, n % 2], c, c, ALU.mult).then_inc(sq_done, 1)

            for n in range(GROUPS):
                centre(n)
                square(n)
            for k in range(1, STAGES):
                pool.wait_ge(p_out[k], all_out[k])

            def gather(n, k, use):
                ready = pool.to_reg(n + 1)
                pool.wait_ge(p_out[0], all_out[0])
                pool.wait_ge(idx_ready, ready)
                for j in range(chunks_of(n)):
                    nc.gpsimd.indirect_dma_start(
                        out=g[:, k, j * HID:(j + 1) * HID], out_offset=None, in_=p_table,
                        in_offset=bass.IndirectOffsetOnAxis(ap=idx[:, k, j:j + 1], axis=0)).then_inc(gathered[k], 16)

            def general():
                first_rows_in(pool)

                def gather_general(n):
                    ready = pool.to_reg(n + 1)
                    pool.wait_ge(p_out[0], all_out[0])
                    pool.wait_ge(rows_ready, ready)
                    for j in range(4):
                        nc.gpsimd.indirect_dma_start(
                            out=g[:, 0, j * HID:(j + 1) * HID], out_offset=None, in_=p_table,
                            in_offset=bass.IndirectOffsetOnAxis(ap=idx[:, 0, j:j + 1], axis=0)).then_inc(rows_in, 16)

                with pool.Fori(0, QUADS) as n:
                    gather_general(n)

            for n in range(RING):
                gather(n, n, 0)
            if_one_window(pool, lambda: rounds(pool, RING, QUADS, gather), general)

            for m, b in enumerate(SHARED):
                s = slice(BT * b, BT * (b + 1))
                pool.wait_ge(scaled_done, BT * (m + 1))
                nc.gpsimd.tensor_tensor(xs[:, s, :], xs[:, s, :], scaled[:, m], ALU.add).then_inc(added_done, 1)

        @block.scalar
        def _(act):
            nc.scalar.preload_act_table(ACT.Sqrt)
            act.dma_start(b1_all[:, :], b1.rearrange("(o h) -> o h", o=1).to_broadcast([NP, HID])).then_inc(b1_in, 16)
            act.wait_ge(w1_zero, 2)
            for half in (0, 1):
                act.dma_start(w1[FEAT * half:FEAT * (half + 1), half, :, :],
                              W1.rearrange("(a f) h -> f a h", a=2)).then_inc(w_in, 16)
            act.dma_start(w2[:, 0:FEAT], W2).then_inc(w2_in, 16)
            act.wait_ge(b2_zero, 1)
            act.dma_start(b2_row[:, 0:FEAT], b2.rearrange("(o f) -> o f", o=1)).then_inc(b2_in, 16)

            def root_of(n):
                act.wait_ge(ss_done, n + 1)
                nc.scalar.activation(stats[:, n % 2, 1, :], stats[:, n % 2, 0, :], ACT.Sqrt, bias=eps[:, :],
                                     scale=1.0 / FEAT).then_inc(std_done, 1)

            def ht_of(n):
                act.wait_ge(ht_psum, n + 1)
                nc.scalar.copy(ht[n][:, 0:4, :],
                               h_bank[0][:, 0:4 * NP].rearrange("p (i n) -> p i n", i=4)).then_inc(ht_done, 1)
                nc.scalar.copy(ht[n][:, 4, :], h_bank[1][:, 0:NP]).then_inc(ht_done, 1)

            def p_of(n):
                act.wait_ge(p_psum, n + 1)
                if n >= STAGES:
                    act.wait_ge(p_out[n % STAGES], 32 * (n // STAGES))
                for m, t, w in parts(GT):
                    nc.scalar.copy(stage[n % STAGES][:, t:t + w, :],
                                   rows_bank[n % 2][m][0:NP, 0:HID * w].rearrange("p (t h) -> p t h", t=w))\
                        .then_inc(p_staged, 1)

            act.wait_ge(eps_there, 1)
            root_of(0)

            for t in range(QT):
                act.wait_ge(src_psum, t + 1)
                nc.scalar.copy(columns_of(src_e, t), tile_of(bank[2 + t])).then_inc(src_table, 1)

            for n in range(GROUPS + 2):
                if 1 <= n < GROUPS:
                    root_of(n)
                if 1 <= n <= GROUPS:
                    ht_of(n - 1)
                if n >= 2:
                    p_of(n - 2)
            act.wait_ge(src_table, QT)
            for n in range(RING):
                nc.scalar.copy(idx[:, n, :], src_e[:, n * 4:n * 4 + 4]).then_inc(idx_ready, 1)

            act.wait_ge(base_psum, 1)
            nc.scalar.copy(base[:, :], bank[0][:, :]).then_inc(base_done, 1)

            act.wait_ge(dst_table, QT)
            act.wait_ge(zeroed, 1)
            nc.scalar.copy(acc[:, :], zeros[:, 0:1].to_broadcast([128, ACOLS])).then_inc(v_zero, 1)

            for credit in (member16_done, spread_done, r_done, c_copied, u_copied):
                act.sem_inc(credit, RING)

            def indices_of(n, k):
                act.wait_ge(z_done, done(n - RING))
                nc.scalar.copy(idx[:, k, :], src_e[:, bass.ds(n * 4, 4)]).then_inc(idx_ready, 1)

            def spread_of(n, k, use):
                act.wait_ge(t_psum, done(n))
                act.wait_ge(zq_done, done(n - 2))
                w = 128 * chunks_of(n)
                nc.scalar.copy(spread[:, k % 2, :, :].rearrange("p c e -> p (c e)")[:, 0:w],
                               t_bank[k % 2][:, 0:w]).then_inc(spread_done, 1)

            def copy_counts(n, k, use):
                act.wait_ge(c_psum, done(n))
                act.wait_ge(v_psum, done(n - 4))
                act.wait_ge(c_done, done(n - 4))
                nc.scalar.copy(sums_c[:, k % 4, :], c_bank[k % 2][0:1, 0:WIN]).then_inc(c_copied, 1)

            def copy_sums(n, k, use):
                act.wait_ge(u_psum, done(n))
                act.wait_ge(v_psum, done(n - 2))
                nc.scalar.copy(sums_u[:, k % 2, :], u_bank[k % 2][:, 0:WIN]).then_inc(u_copied, 1)

            def relu(n, k, use):
                w = HID * chunks_of(n)
                act.wait_ge(z_done, done(n))
                act.wait_ge(u_psum, done(n - 2))
                nc.scalar.activation(r[:, k % 2, 0:w], z[:, k % 2, 0:w], ACT.Relu).then_inc(r_done, 1)

            def member16_of(n, k, use):
                act.wait_ge(member_done, done(n))
                act.wait_ge(u_psum, done(n - MEMBERS))
                c = chunks_of(n)
                nc.scalar.copy(member16[:, k % MEMBERS, 0:c, :],
                               member[:, k % MEMBERS, 0:c, :]).then_inc(member16_done, 1)

            def quads(n, k, use):
                here = isinstance(n, int)
                if not here or RING <= n + LEAD < QUADS:
                    indices_of(n + LEAD, (k + LEAD) % RING)
                if here and n == 2:
                    act.wait_ge(q_pad, 16)
                    act.wait_ge(count_zero, 16)
                if not here or 1 <= n <= QUADS:
                    spread_of(n - 1, (k - 1) % RING, 0)
                if here and n == 1:
                    act.wait_ge(span_done_i, 1)
                    act.wait_ge(widest_done, 1)
                if not here or 1 <= n <= QUADS:
                    copy_counts(n - 1, (k - 1) % RING, 0)
                if not here or 3 <= n <= QUADS + 2:
                    copy_sums(n - 3, (k - 3) % RING, 0)
                if not here or 2 <= n <= QUADS + 1:
                    relu(n - 2, (k - 2) % RING, 0)
                if not here or n < QUADS:
                    member16_of(n, k, 0)

            def fast():
                for n in range(LAG):
                    quads(n, n, 0)
                rounds(act, LAG, QUADS - LEAD, quads)
                for n in range(QUADS - LEAD, QUADS + LAG):
                    quads(n, n % RING, n // RING)

            def general():
                first_rows_in(act)

                def indices_general(n):
                    act.wait_ge(rows_used, n + 1)
                    nc.scalar.copy(idx[:, 0, :], src_e[:, bass.ds(n * 4, 4)]).then_inc(rows_ready, 1)

                def window_general(n, j, m):
                    act.wait_ge(m_made, m)
                    nc.scalar.copy(member16[:, 0, :, :], member[:, 0, :, :]).then_inc(m_copied, 1)
                    act.wait_ge(m_turned, m)
                    nc.scalar.copy(spread[:, 0, :, :].rearrange("p c e -> p (c e)"), t_bank[0][:, 0:512])\
                        .then_inc(m_spread, 1)
                    act.wait_ge(z_made, m)
                    nc.scalar.activation(r[:, 0, :], z[:, 0, :], ACT.Relu).then_inc(r_made, 1)
                    act.wait_ge(u_made, m)
                    nc.scalar.copy(sums_u[:, 0, :], u_bank[0][:, 0:WIN]).then_inc(u_moved, 1)
                    nc.scalar.copy(sums_c[:, 0, :], c_bank[0][0:1, 0:WIN]).then_inc(c_moved, 1)

                items(act, indices_general, window_general)

            if_one_window(act, fast, general)

            act.wait_ge(inverse_done, 1)
            for m, b in enumerate(SHARED):
                act.wait_ge(o_psum, b + 1)
                for t in range(BT):
                    nc.scalar.activation(scaled[:, m, t, :], bank[b % 8][0:NP, 128 * t:128 * t + FEAT], ACT.Copy,
                                         scale=inverse[:, BT * b + t:BT * b + t + 1]).then_inc(scaled_done, 1)

        @block.vector
        def _(dve):
            def mean_of(n):
                s = slice(n * GT, (n + 1) * GT)
                dve.wait_ge(x_in[n * GT // XT], 32)
                nc.vector.tensor_reduce(total[:, s], xs[:, s, :], AX.X, ALU.add).then_inc(total_done, 1)
                dve.wait_ge(total_done, n + 1)
                nc.vector.tensor_scalar(mean[:, s], total[:, s], 1.0 / FEAT, None, ALU.mult).then_inc(mean_done, 1)

            def sum_squares(n):
                dve.wait_ge(sq_done, n + 1)
                nc.vector.tensor_reduce(stats[:, n % 2, 0, :], squares[:, n % 2], AX.X, ALU.add).then_inc(ss_done, 1)

            def normalise(n):
                std, rstd = stats[:, n % 2, 1, :], stats[:, n % 2, 2, :]
                dve.wait_ge(std_done, n + 1)
                nc.vector.reciprocal(rstd, std).then_inc(rstd_done, 1)
                dve.wait_ge(rstd_done, n + 1)
                if n >= HS:
                    dve.wait_ge(ht_psum, n - HS + 1)
                nc.vector.scalar_tensor_tensor(hs[n % HS], centred[n % CENTRED], 0.0,
                                               rstd.unsqueeze(2).to_broadcast([NP, GT, FEAT]),
                                               ALU.max, ALU.mult).then_inc(h_done, 1)

            def rel_of(t):
                dve.wait_ge(dst_psum, t + 1)
                w = base[:, 128 * t:128 * (t + 1)].rearrange("e (o q) -> e o q", o=1)
                nc.vector.tensor_tensor(columns_of(rel_e, t), tile_of(bank[t % 2]), w.to_broadcast([128, 4, 128]),
                                        ALU.subtract).then_inc(dst_table, 1)

            def smallest():
                dve.wait_ge(dst_in, 48)
                nc.vector.tensor_copy(dst_f, dst_i).then_inc(dst_cast, 1)
                nc.vector.tensor_reduce(low[:, :], dst_i, AX.X, ALU.min).then_inc(low_done, 1)

            def largest():
                dve.wait_ge(dst_cast, 1)
                nc.vector.tensor_reduce(high[:, 0:QT - 1], dst_f[:, 0:QT - 1, :], AX.X, ALU.max)
                nc.vector.scalar_tensor_tensor(real[:, :], dst_f[:, QT - 1, :], float(PAD), dst_f[:, QT - 1, :],
                                               ALU.is_lt, ALU.mult).then_inc(real_done, 1)

            def spans():
                dve.wait_ge(real_done, 1)
                nc.vector.tensor_reduce(high[:, QT - 1:QT], real[:, :], AX.X, ALU.max).then_inc(high_done, 1)
                dve.wait_ge(high_done, 1)
                nc.vector.tensor_tensor(span[:, :], high[:, :], low[:, :], ALU.subtract).then_inc(span_done, 1)

            mean_of(0)
            mean_of(1)
            dve.wait_ge(src_in, 48)
            nc.vector.tensor_copy(src_f, src_i).then_inc(src_cast, 1)
            for n in range(GROUPS + 1):
                if n < GROUPS:
                    sum_squares(n)
                if n + 2 < GROUPS:
                    mean_of(n + 2)
                if n < EARLY:
                    normalise(n)
                if n > EARLY:
                    normalise(n - 1)
            smallest()
            largest()
            spans()

            dve.wait_ge(span_psum, 1)
            nc.vector.tensor_copy(spans_i[:, :], bank[1][0:1, :]).then_inc(span_done_i, 1)
            dve.wait_ge(span_done_i, 1)
            nc.vector.tensor_reduce(widest[:, :], spans_i[:, 0:QUADS], AX.X, ALU.max).then_inc(widest_done, 1)
            dve.wait_ge(base_done, 1)
            nc.vector.tensor_copy(base_i[:, :], base[0:1, :]).then_inc(windows, 1)

            dve.wait_ge(b1_in, 16)
            for n in range(GROUPS):
                dve.wait_ge(q_psum, n + 1)
                k = (GROUPS + n) % STAGES
                if n < STAGES:
                    dve.wait_ge(p_out[k], all_out[k])
                else:
                    dve.wait_ge(q_out[k], 32 * (n // STAGES))
                for m, t, w in parts(GT):
                    nc.vector.tensor_tensor(stage[k][:, t:t + w, :],
                                            rows_bank[n % 2][m][0:NP, 0:HID * w].rearrange("p (t h) -> p t h", t=w),
                                            b1_all[:, :].unsqueeze(1).to_broadcast([NP, w, HID]),
                                            ALU.add).then_inc(q_staged, 1)
                if n < QT:
                    rel_of(n)

            for credit in (member_done, z_done, v_done, c_done):
                dve.sem_inc(credit, RING)

            def members_of(n, k, use):
                dve.wait_ge(u_psum, done(n - MEMBERS))
                dve.wait_ge(member16_done, done(n - MEMBERS))
                for j in range(chunks_of(n)):
                    last = nc.vector.tensor_scalar(member[:, k % MEMBERS, j, :], columns[:, :],
                                                   rel_e[:, bass.ds(n * 4 + j, 1)], None, ALU.is_equal)
                last.then_inc(member_done, 1)

            def add_rows(n, k, use):
                w = HID * chunks_of(n)
                dve.wait_ge(zq_done, done(n))
                dve.wait_ge(gathered[k], use * 64 + 16 * chunks_of(n))
                dve.wait_ge(r_done, done(n - 2))
                nc.vector.tensor_tensor(z[:, k % 2, 0:w], z_bank[k % 2][:, 0:w], g[:, k, 0:w],
                                        ALU.add).then_inc(z_done, 1)

            def window_of(n, of):
                at = dve.value_load(base_i[0:1, bass.ds(n, 1)], min_val=0, max_val=NODES - 1)
                return of[:, bass.ds(at, WIN)]

            def add_counts(n, k, use):
                c = window_of(n, count)
                dve.wait_ge(c_copied, done(n))
                dve.wait_ge(c_done, done(n - 1))
                nc.vector.tensor_tensor(c, c, sums_c[:, k % 4, :], ALU.add).then_inc(c_done, 1)

            def add_products(n, k, use):
                v = window_of(n, acc)
                dve.wait_ge(v_psum, done(n))
                dve.wait_ge(v_done, done(n - 1))
                nc.vector.tensor_tensor(v, v, u_bank[k % 2][:, 2 * WIN:3 * WIN], ALU.add).then_inc(v_done, 1)

            def scales():
                dve.wait_ge(count_in, 16)
                nc.vector.tensor_scalar(most[:, :], count_t[:, :], 1.0, None, ALU.max).then_inc(most_done, 1)
                dve.wait_ge(most_done, 1)
                nc.vector.reciprocal(inverse[:, :], most[:, :]).then_inc(inverse_done, 1)

            def quads(n, k, use):
                here = isinstance(n, int)
                if not here or n < QUADS:
                    members_of(n, k, 0)
                if here and n == 1:
                    dve.wait_ge(count_zero, 16)
                if not here or 1 <= n <= QUADS:
                    add_counts(n - 1, (k - 1) % RING, 0)
                if not here or 2 <= n <= QUADS + 1:
                    add_rows(n - 2, (k - 2) % RING, use - (1 if k < 2 else 0))
                if here and n == QUADS + 1:
                    scales()
                if here and n == 4:
                    dve.wait_ge(v_zero, 1)
                if not here or n >= 4:
                    add_products(n - 4, (k - 4) % RING, 0)

            def fast():
                for n in range(LAG):
                    quads(n, n, 0)
                rounds(dve, LAG, QUADS - LEAD, quads)
                for n in range(QUADS - LEAD, QUADS + LAG):
                    quads(n, n % RING, n // RING)

            def general():
                first_rows_in(dve)
                dve.wait_ge(span_done_i, 1)
                nc.vector.tensor_scalar(windows_of[:, :], spans_i[:, :], WIN.bit_length() - 1, None,
                                        ALU.arith_shift_right).then_inc(windows_shifted, 1)
                dve.wait_ge(windows_shifted, 1)
                nc.vector.tensor_scalar(windows_of[:, :], windows_of[:, :], 1, None, ALU.add)\
                    .then_inc(windows_counted, 1)
                dve.wait_ge(count_zero, 16)
                dve.wait_ge(v_zero, 1)
                dve.sem_inc(item_done, 1)
                dve.sem_inc(rows_used, 1)

                def window_general(n, j, m):
                    low_n = dve.value_load(base_i[0:1, bass.ds(n, 1)], min_val=0, max_val=NODES - 1)
                    at = window_start(dve, low_n, j)
                    v, c = acc[:, bass.ds(at, WIN)], count[:, bass.ds(at, WIN)]
                    gathers = dve.to_reg((n + 1) * 64)
                    dve.wait_ge(item_done, m)
                    for k in range(4):
                        last = nc.vector.tensor_scalar(member[:, 0, k, :], columns[:, :], shift[:, bass.ds(j, 1)],
                                                       rel_e[:, bass.ds(n * 4 + k, 1)], ALU.add, ALU.is_equal)
                    last.then_inc(m_made, 1)
                    dve.wait_ge(q_spread, m)
                    dve.wait_ge(rows_in, gathers)
                    nc.vector.tensor_tensor(z[:, 0, :], z_bank[0][:, :], g[:, 0, :], ALU.add).then_inc(z_made, 1)
                    dve.wait_ge(v_made, m)
                    nc.vector.tensor_tensor(v, v, u_bank[0][:, 2 * WIN:3 * WIN], ALU.add).then_inc(v_added, 1)
                    dve.wait_ge(v_added, m)
                    nc.vector.tensor_tensor(c, c, sums_c[:, 0, :], ALU.add).then_inc(item_done, 1)

                def quad_done(n):
                    dve.sem_inc(rows_used, 1)

                dve.wait_ge(item_done, items(dve, None, window_general, quad_done))
                dve.sem_inc(all_added, 1)
                scales()

            if_one_window(dve, fast, general)

            dve.wait_ge(inverse_done, 1)
            for b in range(BATCHES):
                if b in SHARED:
                    continue
                dve.wait_ge(o_psum, b + 1)
                for t in range(BT * b, BT * (b + 1)):
                    nc.vector.scalar_tensor_tensor(xs[:, t, :], bank[b % 8][0:NP, 128 * (t % BT):128 * (t % BT) + FEAT],
                                                   inverse[:, t:t + 1], xs[:, t, :],
                                                   ALU.mult, ALU.add).then_inc(res_done, 1)

        @block.tensor
        def _(pe):
            def transposed(table, t, to, psum):
                for c in range(4):
                    last = nc.tensor.transpose(to[:, 128 * c:128 * (c + 1)], table[:, t, 128 * c:128 * (c + 1)],
                                               ident[:, :])
                last.then_inc(psum, 1)

            pe.wait_ge(consts, 5)
            pe.wait_ge(src_cast, 1)
            for t in range(QT):
                transposed(src_f, t, bank[2 + t], src_psum)

            def transpose_h(n):
                pe.wait_ge(h_done, n + 1)
                if n:
                    pe.wait_ge(ht_done, 2 * n)
                for i in range(GT // 2):
                    last = nc.tensor.transpose(h_bank[i // 4][:, NP * (i % 4):NP * (i % 4 + 1)],
                                               hs[n % HS][:, 2 * i:2 * i + 2, :].rearrange("p t f -> p (t f)"),
                                               ident[0:NP, 0:NP])
                last.then_inc(ht_psum, 1)

            def products(n, half, psum):
                for t in range(GT):
                    last = nc.tensor.matmul(rows_bank[n % 2][t // 4][0:NP, HID * (t % 4):HID * (t % 4 + 1)],
                                            ht[n][:, t // 2, :], w1[:, t % 2, half, :], start=True, stop=True)
                last.then_inc(psum, 1)

            def spans_and_starts():
                pe.wait_ge(span_done, 1)
                for t in range(QT):
                    last = nc.tensor.matmul(bank[1][0:1, 128 * t:128 * (t + 1)], span[:, t:t + 1], ident[:, :],
                                            start=True, stop=True)
                last.then_inc(span_psum, 1)
                for t in range(QT):
                    last = nc.tensor.matmul(bank[0][:, 128 * t:128 * (t + 1)], low[:, t:t + 1].to_broadcast([128, 128]),
                                            ident[:, :], start=True, stop=True)
                last.then_inc(base_psum, 1)

            pe.wait_ge(w_in, 32)
            for n in range(GROUPS + 1):
                if 1 != n < GROUPS:
                    transpose_h(n)
                if n:
                    if n == 1:
                        pe.wait_ge(src_table, QT)
                    pe.wait_ge(ht_done, 2 * n)
                    if n > 2:
                        pe.wait_ge(p_staged, 3 * (n - 2))
                    products(n - 1, 0, p_psum)
                if n == GROUPS:
                    spans_and_starts()
                if n == 1:
                    transpose_h(1)
            for n in range(GROUPS):
                if n < 2:
                    pe.wait_ge(p_staged, 3 * (GROUPS - 1 + n))
                else:
                    pe.wait_ge(q_staged, 3 * (n - 1))
                products(n, 1, q_psum)
                if n < QT:
                    if n < 2:
                        pe.wait_ge(*((base_done, 1), (span_done_i, 1))[n])
                    else:
                        pe.wait_ge(dst_table, n - 1)
                    transposed(dst_f, n, bank[n % 2], dst_psum)

            pe.wait_ge(w2_in, 16)
            pe.wait_ge(b2_in, 16)
            pe.wait_ge(q_staged, 3 * GROUPS)
            for credit in (t_psum, c_psum, zq_done, u_psum, v_psum):
                pe.sem_inc(credit, RING)

            def spread_q(n, k, use):
                pe.wait_ge(spread_done, done(n))
                pe.wait_ge(window_in[k], use * 16 + 16)
                pe.wait_ge(z_done, done(n - 2))
                for j in range(chunks_of(n)):
                    last = nc.tensor.matmul(z_bank[k % 2][:, HID * j:HID * (j + 1)], spread[:, k % 2, j, :],
                                            qw[:, k, :], start=True, stop=True)
                last.then_inc(zq_done, 1)

            def sum_edges(n, k, use):
                pe.wait_ge(r_done, done(n))
                pe.wait_ge(v_done, done(n - 2))
                sums = u_bank[k % 2]
                chunks = chunks_of(n)
                for c in range(chunks):
                    last = nc.tensor.matmul(sums[:, 0:WIN], r[:, k % 2, HID * c:HID * (c + 1)],
                                            member[:, k % MEMBERS, c, :], start=c == 0, stop=c == chunks - 1)
                last.then_inc(u_psum, 1)

            def transpose_members(n, k, use):
                pe.wait_ge(member16_done, done(n))
                pe.wait_ge(spread_done, done(n - 2))
                for c in range(chunks_of(n)):
                    last = nc.tensor.transpose(t_bank[k % 2][:, 128 * c:128 * (c + 1)], member16[:, k % MEMBERS, c, :],
                                               ident16[:, :])
                last.then_inc(t_psum, 1)
                pe.wait_ge(c_copied, done(n - 2))
                for c in range(chunks_of(n)):
                    last = nc.tensor.matmul(c_bank[k % 2][0:1, 0:WIN], ones16[:, :], member16[:, k % MEMBERS, c, :],
                                            start=c == 0, stop=c == chunks_of(n) - 1)
                last.then_inc(c_psum, 1)

            def to_v(k, of_sums, of_counts):
                nc.tensor.matmul(u_bank[k][:, 2 * WIN:3 * WIN], w2[:, :], of_sums, start=True, stop=False)
                return nc.tensor.matmul(u_bank[k][:, 2 * WIN:3 * WIN], b2_row[:, :], of_counts, start=False, stop=True)

            def add_to_v(n, k, use):
                pe.wait_ge(u_copied, done(n))
                pe.wait_ge(c_copied, done(n))
                to_v(k % 2, sums_u[:, k % 2, :], sums_c[:, k % 4, :]).then_inc(v_psum, 1)

            def quads(n, k, use):
                here = isinstance(n, int)
                if not here or 1 <= n <= QUADS:
                    spread_q(n - 1, (k - 1) % RING, use - (0 if k else 1))
                if not here or 2 <= n <= QUADS + 1:
                    sum_edges(n - 2, (k - 2) % RING, 0)
                if not here or n < QUADS:
                    transpose_members(n, k, 0)
                if not here or 3 <= n <= QUADS + 2:
                    add_to_v(n - 3, (k - 3) % RING, 0)

            def fast():
                for n in range(LAG):
                    quads(n, n, 0)
                rounds(pe, LAG, QUADS - LEAD, quads)
                for n in range(QUADS - LEAD, QUADS + LAG):
                    quads(n, n % RING, n // RING)
                pe.wait_ge(v_done, done(QUADS - 1))
                pe.wait_ge(c_done, done(QUADS - 1))

            def general():
                def window_general(n, j, m):
                    loads = pe.to_reg(m * 16)
                    pe.wait_ge(m_copied, m)
                    for c in range(4):
                        last = nc.tensor.transpose(t_bank[0][:, 128 * c:128 * (c + 1)], member16[:, 0, c, :],
                                                   ident16[:, :])
                    last.then_inc(m_turned, 1)
                    pe.wait_ge(m_spread, m)
                    pe.wait_ge(w_loaded, loads)
                    for c in range(4):
                        last = nc.tensor.matmul(z_bank[0][:, HID * c:HID * (c + 1)], spread[:, 0, c, :], qw[:, 0, :],
                                                start=True, stop=True)
                    last.then_inc(q_spread, 1)
                    pe.wait_ge(r_made, m)
                    for c in range(4):
                        nc.tensor.matmul(u_bank[0][:, 0:WIN], r[:, 0, HID * c:HID * (c + 1)], member[:, 0, c, :],
                                         start=c == 0, stop=c == 3)
                    for c in range(4):
                        last = nc.tensor.matmul(c_bank[0][0:1, 0:WIN], ones16[:, :], member16[:, 0, c, :],
                                                start=c == 0, stop=c == 3)
                    last.then_inc(u_made, 1)
                    pe.wait_ge(u_moved, m)
                    pe.wait_ge(c_moved, m)
                    to_v(0, sums_u[:, 0, :], sums_c[:, 0, :]).then_inc(v_made, 1)

                items(pe, None, window_general)
                pe.wait_ge(all_added, 1)

            if_one_window(pe, fast, general)

            for b in range(BATCHES):
                if b >= 8:
                    if b - 8 in SHARED:
                        pe.wait_ge(scaled_done, BT * shared(b - 7))
                    else:
                        pe.wait_ge(res_done, BT * (b - 7 - shared(b - 7)))
                for t in range(BT):
                    node = slice(BT * b + t, BT * b + t + (NP - 1) * NT + 1, NT)
                    last = nc.tensor.transpose(bank[b % 8][0:NP, 128 * t:128 * (t + 1)], acc[:, node], ident[:, :])
                last.then_inc(o_psum, 1)


_INS = ["x", "src", "dst", "L0_gnn_W1", "L0_gnn_b1", "L0_gnn_W2", "L0_gnn_b2"]


def kernel(**inputs):
    import numpy as _np
    import concourse.bacc as _bacc
    from concourse import mybir as _mybir
    from concourse.bass_utils import run_bass_kernel_spmd as _run

    nc = _bacc.Bacc("TRN2", target_bir_lowering=False, num_devices=1)
    arrays, args = {}, []
    for name in _INS:
        a = _np.ascontiguousarray(inputs[name])
        arrays[f"in_{name}_dram"] = a
        args.append(nc.dram_tensor(f"in_{name}_dram", a.shape, _mybir.dt.from_np(a.dtype), kind="ExternalInput").ap())
    out = nc.dram_tensor("out_0_dram", [NODES, FEAT], F32, kind="ExternalOutput").ap()
    gnn_kernel(nc, *args, out)
    r = _run(nc, [arrays], core_ids=[0])
    return r.results[0]["out_0_dram"]
```
